# Optimizing a Trainium2 kernel written in Bass

```python
import numpy as np
import jax
import jax.numpy as jnp

def _softmax(x, axis=-1):
    return jax.nn.softmax(x, axis=axis)

def _gelu(x):
    return jax.nn.gelu(x, approximate=True)

def _silu(x):
    return jax.nn.silu(x)

def _sigmoid(x):
    return jax.nn.sigmoid(x)

def _layernorm(x, axis=-1, eps=1e-05):
    m = jnp.mean(x, axis=axis, keepdims=True)
    v = jnp.var(x, axis=axis, keepdims=True)
    return (x - m) / jnp.sqrt(v + eps)

def _scatter_add(tgt, idx, src, axis=0):
    return tgt.at[idx].add(src)

def _segment_sum(src, seg, n):
    return jax.ops.segment_sum(src, seg, n)
kernel_name = 'mk_decoder_postln_d1_seqx_r8_1c128d'

def setup_inputs(seed: int=0):
    np.random.seed(seed)
    _w = jnp.asarray

    def _rec_inputs():
        import jax
        import jax.numpy as jnp
        _rk = jax.random.key(seed)
        x = -0.0002928 + 1 * jax.random.normal(jax.random.fold_in(_rk, 1), (32, 64, 128), jnp.float32)
        _lenS = 64 - jax.random.randint(jax.random.fold_in(_rk, 7), (32,), 0, max(1, 64 // 4) + 1, jnp.int32)
        _lenS2 = 64 - jax.random.randint(jax.random.fold_in(_rk, 8), (32,), 0, max(1, 64 // 4) + 1, jnp.int32)
        _ctx_1024P = jax.random.normal(jax.random.fold_in(_rk, 11), (32, 16, 128), jnp.float32)
        _ctx_1024c = jax.random.dirichlet(jax.random.fold_in(_rk, 511), 0.3 * jnp.ones((16,), jnp.float32), (32, 64))
        _ctx_1024t = jnp.einsum('bsk,bkd->bsd', _ctx_1024c, _ctx_1024P)
        _ctx_1024t = _ctx_1024t * jax.lax.rsqrt(jnp.mean(jnp.square(_ctx_1024t)) + 1e-12) * 0.953939
        ctx_1024 = -1.39393e-06 + 0.999914 * (_ctx_1024t + 0.3 * jax.random.normal(jax.random.fold_in(_rk, 611), (32, 64, 128), jnp.float32))
        _validS = jnp.arange(64)[None, :] < _lenS[:, None]
        _validS2 = jnp.arange(64)[None, :] < _lenS2[:, None]
        _causal = jnp.tril(jnp.ones((64, 64), dtype=bool))
        mask_Bx1xSxS2_ik1 = jnp.where(jnp.broadcast_to(_validS2[:, None, None, :], (32, 1, 64, 64)), 1, 0).astype(jnp.int32)
        return (x, ctx_1024, mask_Bx1xSxS2_ik1)
    x, ctx_1024, mask_Bx1xSxS2_ik1 = _rec_inputs()

    def _L0_attn_setup():
        import jax, jax.numpy as jnp
        import numpy as np
        B, S, D, DV = (1, 512, 128, 128)
        key = jax.random.key(seed)
        kq, kk, kv, ks, kp = jax.random.split(key, 5)
        return {'q': jax.random.normal(kq, (B, S, D), dtype=jnp.float32), 'k': jax.random.normal(kk, (B, S, D), dtype=jnp.float32), 'v': jax.random.normal(kv, (B, S, DV), dtype=jnp.float32), 'scale_factor': jax.random.normal(ks, (1,), dtype=jnp.float32), 'dropout_p': jax.random.uniform(kp, (1,), dtype=jnp.float32)}
    _L0_attn_all = _L0_attn_setup()
    _L0_attn_in = {k: v for k, v in _L0_attn_all.items() if k in ('k', 'v', 'scale_factor', 'dropout_p')}
    del _L0_attn_all

    def _L0_xattn_setup():
        import jax, jax.numpy as jnp
        import numpy as np
        import math
        DIM = 128
        NUM_HEADS = 16
        HEAD_DIM = DIM // NUM_HEADS
        ROPE_THETA = 10000.0

        def _rope(x):
            S, D = (x.shape[-2], x.shape[-1])
            inv_freq = 1.0 / ROPE_THETA ** (jnp.arange(0, D, 2, dtype=jnp.float32) / D)
            ang = jnp.arange(S, dtype=jnp.float32)[:, None] * inv_freq[None, :]
            cos, sin = (jnp.cos(ang), jnp.sin(ang))
            x1, x2 = (x[..., 0::2], x[..., 1::2])
            out_even = x1 * cos - x2 * sin
            out_odd = x1 * sin + x2 * cos
            return jnp.stack([out_even, out_odd], axis=-1).reshape(x.shape)
        key = jax.random.key(seed)
        ks = jax.random.split(key, 8)
        B, S = (2, 256)
        sc = 1.0 / math.sqrt(DIM)
        return {'q': jax.random.normal(ks[0], (B, S, DIM), jnp.float32), 'k': jax.random.normal(ks[1], (B, S, DIM), jnp.float32), 'v': jax.random.normal(ks[2], (B, S, DIM), jnp.float32), 'mask': jax.random.randint(ks[3], (B, 1, S, S), 0, 2, jnp.int32), 'Wq': jax.random.normal(ks[4], (DIM, DIM), jnp.float32) * sc, 'Wk': jax.random.normal(ks[5], (DIM, DIM), jnp.float32) * sc, 'Wv': jax.random.normal(ks[6], (DIM, DIM), jnp.float32) * sc, 'Wo': jax.random.normal(ks[7], (DIM, DIM), jnp.float32) * sc, 'bo': jnp.zeros((DIM,), jnp.float32)}
    _L0_xattn_all = _L0_xattn_setup()
    _L0_xattn_in = {k: v for k, v in _L0_xattn_all.items() if k in ('Wq', 'Wk', 'Wv', 'Wo', 'bo')}
    del _L0_xattn_all

    def _L0_ffn_setup():
        import jax, jax.numpy as jnp
        import numpy as np
        D_MODEL = 128
        D_FF = 512
        N_EXPERTS = 8
        INIT_SCALE = 0.1

        def _trunc_normal(key, shape, std):
            return std * jax.random.truncated_normal(key, -2.0, 2.0, shape, dtype=jnp.float32)
        key = jax.random.key(seed)
        ks = jax.random.split(key, 5)
        x = jax.random.normal(ks[0], (4, 128, D_MODEL), dtype=jnp.float32)
        router_W = _trunc_normal(ks[1], (D_MODEL, N_EXPERTS), INIT_SCALE / np.sqrt(D_MODEL))
        router_b = jnp.zeros((N_EXPERTS,), dtype=jnp.float32)
        W1 = _trunc_normal(ks[2], (N_EXPERTS, D_MODEL, D_FF), INIT_SCALE / np.sqrt(D_MODEL))
        b1 = jnp.zeros((N_EXPERTS, D_FF), dtype=jnp.float32)
        W2 = _trunc_normal(ks[3], (N_EXPERTS, D_FF, D_MODEL), INIT_SCALE / np.sqrt(D_FF))
        b2 = jnp.zeros((N_EXPERTS, D_MODEL), dtype=jnp.float32)
        return {'x': x, 'router_W': router_W, 'router_b': router_b, 'W1': W1, 'b1': b1, 'W2': W2, 'b2': b2}
    _L0_ffn_all = _L0_ffn_setup()
    _L0_ffn_in = {k: v for k, v in _L0_ffn_all.items() if k in ('router_W', 'router_b', 'W1', 'b1', 'W2', 'b2')}
    del _L0_ffn_all
    return {'x': x, 'ctx_1024': ctx_1024, 'mask_Bx1xSxS2_ik1': mask_Bx1xSxS2_ik1, 'L0_attn_k': _L0_attn_in['k'], 'L0_attn_v': _L0_attn_in['v'], 'L0_attn_scale_factor': _L0_attn_in['scale_factor'], 'L0_attn_dropout_p': _L0_attn_in['dropout_p'], 'L0_xattn_Wq': _L0_xattn_in['Wq'], 'L0_xattn_Wk': _L0_xattn_in['Wk'], 'L0_xattn_Wv': _L0_xattn_in['Wv'], 'L0_xattn_Wo': _L0_xattn_in['Wo'], 'L0_xattn_bo': _L0_xattn_in['bo'], 'L0_ffn_router_W': _L0_ffn_in['router_W'], 'L0_ffn_router_b': _L0_ffn_in['router_b'], 'L0_ffn_W1': _L0_ffn_in['W1'], 'L0_ffn_b1': _L0_ffn_in['b1'], 'L0_ffn_W2': _L0_ffn_in['W2'], 'L0_ffn_b2': _L0_ffn_in['b2']}

def reference(x, ctx_1024, mask_Bx1xSxS2_ik1, L0_attn_k, L0_attn_v, L0_attn_scale_factor, L0_attn_dropout_p, L0_xattn_Wq, L0_xattn_Wk, L0_xattn_Wv, L0_xattn_Wo, L0_xattn_bo, L0_ffn_router_W, L0_ffn_router_b, L0_ffn_W1, L0_ffn_b1, L0_ffn_W2, L0_ffn_b2):
    import jax
    import jax.numpy as jnp

    def _L0_attn_ref(q, k, v, scale_factor, dropout_p):
        import jax, jax.numpy as jnp
        import numpy as np
        B, S, D, DV = (1, 512, 128, 128)
        b, s, d = q.shape
        step = s // 4
        scale = q[:, ::step].reshape(b, -1)
        qk = jnp.einsum('bsd,btd->bst', q, k)
        scaled_qk = qk * scale[:, None, :]
        softmax_qk = jax.nn.softmax(scaled_qk, axis=-1)
        return jnp.einsum('bst,btv->bsv', softmax_qk, v)

    def _L0_xattn_ref(q, k, v, mask, Wq, Wk, Wv, Wo, bo):
        import jax, jax.numpy as jnp
        import numpy as np
        import math
        DIM = 128
        NUM_HEADS = 16
        HEAD_DIM = DIM // NUM_HEADS
        ROPE_THETA = 10000.0

        def _rope(x):
            S, D = (x.shape[-2], x.shape[-1])
            inv_freq = 1.0 / ROPE_THETA ** (jnp.arange(0, D, 2, dtype=jnp.float32) / D)
            ang = jnp.arange(S, dtype=jnp.float32)[:, None] * inv_freq[None, :]
            cos, sin = (jnp.cos(ang), jnp.sin(ang))
            x1, x2 = (x[..., 0::2], x[..., 1::2])
            out_even = x1 * cos - x2 * sin
            out_odd = x1 * sin + x2 * cos
            return jnp.stack([out_even, out_odd], axis=-1).reshape(x.shape)
        B, S, _ = q.shape
        qh = (q @ Wq).reshape(B, S, NUM_HEADS, HEAD_DIM).transpose(0, 2, 1, 3)
        kh = (k @ Wk).reshape(B, S, NUM_HEADS, HEAD_DIM).transpose(0, 2, 1, 3)
        vh = (v @ Wv).reshape(B, S, NUM_HEADS, HEAD_DIM)
        qh = _rope(qh)
        kh = _rope(kh)
        score = jnp.einsum('nhqd,nhkd->nhqk', qh, kh) / math.sqrt(HEAD_DIM)
        score = jnp.where(mask == 0, jnp.float32(-10000.0), score)
        attn = jax.nn.softmax(score, axis=-1)
        out = jnp.einsum('nhqk,nkhd->nqhd', attn, vh).reshape(B, S, DIM)
        return out @ Wo + bo

    def _L0_ffn_ref(x, router_W, router_b, W1, b1, W2, b2):
        import jax, jax.numpy as jnp
        import numpy as np
        D_MODEL = 128
        D_FF = 512
        N_EXPERTS = 8
        INIT_SCALE = 0.1

        def _trunc_normal(key, shape, std):
            return std * jax.random.truncated_normal(key, -2.0, 2.0, shape, dtype=jnp.float32)
        logits = jnp.einsum('bsd,de->bse', x.astype(jnp.float32), router_W) + router_b
        probs = jax.nn.softmax(logits, axis=-1)
        top1 = jnp.argmax(probs, axis=-1)
        mask = jax.nn.one_hot(top1, N_EXPERTS, dtype=x.dtype)
        gates = mask * probs.astype(x.dtype)
        h = jax.nn.relu(jnp.einsum('bsd,edf->besf', x, W1) + b1[:, None, :])
        y = jnp.einsum('besf,efd->besd', h, W2) + b2[:, None, :]
        out = jnp.einsum('bse,besd->bsd', gates, y)
        return out
    x = _layernorm(x + _L0_attn_ref(x, L0_attn_k, L0_attn_v, L0_attn_scale_factor, L0_attn_dropout_p), axis=-1)
    x = _layernorm(x + _L0_xattn_ref(x, ctx_1024, ctx_1024, mask_Bx1xSxS2_ik1, L0_xattn_Wq, L0_xattn_Wk, L0_xattn_Wv, L0_xattn_Wo, L0_xattn_bo), axis=-1)
    x = _layernorm(x + _L0_ffn_ref(x, L0_ffn_router_W, L0_ffn_router_b, L0_ffn_W1, L0_ffn_b1, L0_ffn_W2, L0_ffn_b2), axis=-1)
    return x

_drawn_inputs = setup_inputs


def setup_inputs(seed=0):
    import zlib

    import numpy as np

    out = dict(_drawn_inputs(seed))
    spreads = {'L0_xattn_bo': (0.0, 0.1),
     'L0_ffn_router_b': (0.0, 0.54),
     'L0_ffn_b1': (0.0, 0.8),
     'L0_ffn_b2': (0.0, 0.544)}
    factors = {'L0_ffn_router_W': 4.932, 'L0_ffn_W1': 8.0, 'L0_ffn_W2': 8.0}
    for name, (base, spread) in spreads.items():
        noise = np.random.default_rng([zlib.crc32(name.encode()), seed]).standard_normal(out[name].shape)
        drawn = base * np.exp(spread * noise) if base else spread * noise
        out[name] = jnp.asarray(drawn.astype(out[name].dtype))
    for name, factor in factors.items():
        out[name] = (out[name] * factor).astype(out[name].dtype)
    return out
```

```python
from contextlib import ExitStack

import concourse.bass as bass
from concourse import mybir

ALU = mybir.AluOpType
ACT = mybir.ActivationFunctionType
AX = mybir.AxisListType
F32 = mybir.dt.float32
BF16 = mybir.dt.bfloat16
I32 = mybir.dt.int32
U32 = mybir.dt.uint32

P = 128
B, S, D = 32, 64, 128
NT = B * S // P
T = 512
TB = T // P
HEADS, HD = 16, 8
HPAIR = HEADS // 2
RG = 4
HG = HEADS // RG
GROUP_KEYS = HG * S
BANK = 512
VA = 2 * (HD + 1)
E, F = 8, 512
FB = F // P
FT = NT + E - 1
RING = 4
VALS = 5
EPS = 1e-5
MASKED = -10000.0

C_ID = 0
C_COS = C_ID + P
C_SIN = C_COS + 2 * P
C_HM = C_SIN + 2 * P
C_VA = C_HM + HG
C_TRI = C_VA + 2 * HPAIR * VA
C_IOTA = C_TRI + P
C_W8 = C_IOTA + P
C_TOK = C_W8 + E
C_ALL = C_TOK + 2 * NT


class Tile:

    def __init__(self, group, place, per=2):
        self.group, self.place, self.per = group, place, per

    @property
    def index(self):
        return self.group * self.per + self.place

    @property
    def done(self):
        return self.index + 1

    @property
    def landed(self):
        return (self.group + 1) * 16


def wait_before(eng, sem, tile, back=1):
    if isinstance(tile.index, int) and tile.index < back:
        return
    eng.wait_ge(sem, tile.index + (1 - back))


def carry(eng, passed):
    eng.sem_inc(passed, 1)


def spread(ap, axis, shape):
    return ap.unsqueeze(axis).to_broadcast(shape)


def decoder_kernel(nc, x_tok, x_t, x_scale, ctx_t, mask, attn_kt, attn_v, wq, wq_swap, wk, wk_swap, wv, wo, bo,
                   router_w, router_b, w1, b1, w2, b2, consts, out):
    with ExitStack() as ctx:
        def sb(name, shape, dt=F32):
            return ctx.enter_context(nc.sbuf_tensor(name, shape, dt))

        def psum(name, shape, dt=F32):
            return ctx.enter_context(nc.psum_tensor(name, shape, dt))

        def sem(name):
            return ctx.enter_context(nc.semaphore(name))

        x2_dram = nc.dram_tensor("x2_rows", [NT * P, D], F32, kind="Internal").ap()

        cst = sb("cst", [P, C_ALL])
        ident = cst[:, C_ID:C_ID + P]
        kt_sb = sb("kt_sb", [P, T])
        v_sb = sb("v_sb", [P, TB, D])
        w_qk = sb("w_qk", [P, 4, D])
        w_v = sb("w_v", [P, D])
        w_o = sb("w_o", [P, D])
        bo_bc = sb("bo_bc", [P, D])
        r_w = sb("r_w", [P, E])
        r_b = sb("r_b", [P, E])

        xt = [sb(f"xt{n}", [P, P]) for n in range(2)]
        xk = [sb(f"xk{n}", [P, D]) for n in range(2)]
        scale_bc = [sb(f"scale_bc{n}", [P, T]) for n in range(2)]
        s_sb = sb("s_sb", [P, T])
        s_max = sb("s_max", [P, 1])
        s_nmax = sb("s_nmax", [P, 1])
        p_sb = sb("p_sb", [P, T])
        p_sum = sb("p_sum", [P, 1])
        p_inv = sb("p_inv", [P, 1])
        pt_sb = sb("pt_sb", [P, T])
        r1 = sb("r1", [P, D])
        st1 = sb("st1", [P, 6])
        mv1 = sb("mv1", [P, 2])
        rstd1 = sb("rstd1", [P, 1])
        x1 = [sb(f"x1_{n}", [P, D]) for n in range(2)]

        ct = [sb(f"ct{n}", [P, 2, P]) for n in range(2)]
        mk = [sb(f"mk{n}", [P, S], I32) for n in range(2)]
        x1b = sb("x1b", [P, D])
        x1t = sb("x1t", [P, P])
        rope_c = sb("rope_c", [P, 2 * P])
        rope_s = sb("rope_s", [P, 2 * P])
        qkt = sb("qkt", [P, 2 * P])
        kbd = sb("kbd", [P, 2, HG, S])
        vaug = sb("vaug", [P, 2 * HPAIR, VA])
        sc_sb = sb("sc_sb", [P, HEADS, S])
        sc_max = sb("sc_max", [P, HEADS])
        sd_sb = sb("sd_sb", [P, HEADS, S])
        pb_sb = sb("pb_sb", [P, HEADS * S])
        pbt = sb("pbt", [P, HEADS * S])
        ao_inv = sb("ao_inv", [P, HEADS])
        ao = sb("ao", [P, HEADS, HD])
        aot = sb("aot", [P, P])
        r2 = sb("r2", [P, D])
        st2 = sb("st2", [P, 6])
        mv2 = sb("mv2", [P, 2])
        rstd2 = sb("rstd2", [P, 1])
        x2 = [sb(f"x2_{n}", [P, D]) for n in range(2)]
        x2t = sb("x2t", [P, P])
        logits = sb("logits", [P, NT, E])
        half_neg = sb("half_neg", [P, 1])
        ve1 = sb("ve1", [P, 1])
        ve2 = sb("ve2", [P, 1])

        tri_bf = sb("tri_bf", [P, P], BF16)
        ones_bf = sb("ones_bf", [P, P], BF16)
        lg_max = sb("lg_max", [P, NT])
        lg_exp = sb("lg_exp", [P, NT, E])
        lg_sub = sb("lg_sub", [P, NT, E])
        gate = sb("gate", [P, NT])
        gate_rest = sb("gate_rest", [P, NT])
        at_max = sb("at_max", [P, NT, E])
        first = sb("first", [P, NT])
        chosen = sb("chosen", [P, NT, E])
        chosen_bf = sb("chosen_bf", [P, NT, E], BF16)
        whole = sb("whole", [P, E])
        whole_i = sb("whole_i", [P, E], I32)
        ends = sb("ends", [P, E])
        starts = sb("starts", [P, E])
        place_e = sb("place_e", [P, NT, E])
        place_f = sb("place_f", [P, NT])
        place_i = sb("place_i", [P, NT], I32)
        part_i = sb("part_i", [P, NT], I32)
        lane_f = sb("lane_f", [P, NT])
        tile_f = sb("tile_f", [P, NT])
        lane_hot = sb("lane_hot", [P, NT, P], BF16)
        tile_hot = sb("tile_hot", [P, NT, FT], BF16)
        vals = sb("vals", [P, NT, VALS], BF16)
        tile_vals = sb("tile_vals", [P, NT, VALS, FT], BF16)
        sorted_sb = sb("sorted_sb", [P, VALS, FT])
        row_f = sb("row_f", [P, FT])
        from_f = sb("from_f", [P, FT])
        to_f = sb("to_f", [P, FT])
        from_row = sb("from_row", [P, FT], U32)
        to_row = sb("to_row", [P, FT], U32)
        gate_sum = sb("gate_sum", [P, FT])
        sorted_gate = sb("sorted_gate", [P, FT])
        past = sb("past", [P, FT, E])
        expert_f = sb("expert_f", [P, FT])
        expert_low = sb("expert_low", [P, FT])
        expert_of = sb("expert_of", [P, FT], I32)

        w1_sb = sb("w1_sb", [P, E * F])
        w2_sb = sb("w2_sb", [P, E * FB * D])
        b1_bc = sb("b1_bc", [P, E * F])
        b2_bc = sb("b2_bc", [P, E * D])
        from_cur = [sb(f"from_cur{n}", [P, 1], U32) for n in range(RING)]
        to_cur = [sb(f"to_cur{n}", [P, 1], U32) for n in range(RING)]
        xs = [sb(f"xs{n}", [P, D]) for n in range(RING)]
        xst = [sb(f"xst{n}", [P, P]) for n in range(2)]
        h_sb = [sb(f"h_sb{n}", [P, F]) for n in range(2)]
        ht_sb = [sb(f"ht_sb{n}", [P, F]) for n in range(2)]
        yb = sb("yb", [P, D])
        r3 = [sb(f"r3_{n}", [P, D]) for n in range(2)]
        st3 = sb("st3", [P, 6])
        mv3 = [sb(f"mv3_{n}", [P, 2]) for n in range(2)]
        ve3 = sb("ve3", [P, 1])
        rstd3 = [sb(f"rstd3_{n}", [P, 1]) for n in range(2)]
        res = [sb(f"res{n}", [P, D]) for n in range(RING)]

        ps_s = psum("ps_s", [P, BANK])
        ps_pt = psum("ps_pt", [P, BANK])
        ps_bt = psum("ps_bt", [P, 2 * BANK])
        ps_sc = psum("ps_sc", [P, RG, BANK])
        sc_view = ps_sc[:, :, 0:GROUP_KEYS]
        ps_o = ps_pt[:, 0:D]
        ps_x1t = ps_sc[:, 0, 384:512]
        ps_qk = ps_sc[:, 1, 256:512]
        ps_sw = ps_sc[:, 2, 256:512]
        ps_v = ps_sc[:, 3, 256:512]
        ps_bo = ps_sc[:, 1, 256:256 + HPAIR * VA]
        ps_aot = ps_sc[:, 2, 256:384]
        ps_wo = ps_sc[:, 2, 384:512]
        ps_x2t = ps_sc[:, 3, 256:384]
        ps_log = ps_sc[:, 3, 384:384 + E]

        ps_rank = ps_sc[:, 0, 0:NT * E]
        ps_count = ps_sc[:, 1, 0:E]
        ps_sorted = ps_sc[:, 2, 0:VALS * FT]
        ps_h = [ps_s[:, :], ps_pt[:, :]]
        ps_ht = [ps_bt[:, 0:F], ps_bt[:, F:2 * F]]
        ps_xs = ps_sc[:, 3, 0:P]
        ps_y = [ps_sc[:, 0, 0:D], ps_sc[:, 1, 0:D]]

        consts_in = sem("consts_in")
        weights_in = sem("weights_in")
        pool_ones = sem("pool_ones")
        route = sem("route")
        shifted = sem("shifted")
        exp_ready = sem("exp_ready")
        chosen_ready = sem("chosen_ready")
        rank_ready = sem("rank_ready")
        hot_ready = sem("hot_ready")
        sorted_ready = sem("sorted_ready")
        routed = sem("routed")
        xs_in = [sem(f"xs_in{n}") for n in range(RING)]
        from_copied = sem("from_copied")
        to_copied = sem("to_copied")
        xst_ready = sem("xst_ready")
        xst_copied = sem("xst_copied")
        h_ready = sem("h_ready")
        h_added = sem("h_added")
        ht_ready = sem("ht_ready")
        ht_copied = sem("ht_copied")
        y_ready = sem("y_ready")
        yb_ready = sem("yb_ready")
        r3_ready = sem("r3_ready")
        st3_ready = sem("st3_ready")
        var3_ready = sem("var3_ready")
        ve3_ready = sem("ve3_ready")
        rstd3_ready = sem("rstd3_ready")
        res_ready = sem("res_ready")
        out_stored = [sem(f"out_stored{n}") for n in range(RING)]
        x_in = [sem(f"x_in{n}") for n in range(2)]
        ctx_in = [sem(f"ctx_in{n}") for n in range(2)]
        s_ready = sem("s_ready")
        s_scaled = sem("s_scaled")
        nmax_ready = sem("nmax_ready")
        p_ready = sem("p_ready")
        pt_ready = sem("pt_ready")
        pt_copied = sem("pt_copied")
        o_ready = sem("o_ready")
        var1_ready = sem("var1_ready")
        ve1_ready = sem("ve1_ready")
        rstd1_ready = sem("rstd1_ready")
        x1_ready = sem("x1_ready")
        x1b_ready = sem("x1b_ready")
        x1t_ready = sem("x1t_ready")
        x1t_copied = sem("x1t_copied")
        kv_ready = sem("kv_ready")
        q_ready = sem("q_ready")
        v_copied = sem("v_copied")
        rope_ready = sem("rope_ready")
        qk_ready = sem("qk_ready")
        kbd_ready = sem("kbd_ready")
        sc_filled = sem("sc_filled")
        sc_ready = sem("sc_ready")
        sc_masked = sem("sc_masked")
        scmax_ready = sem("scmax_ready")
        sd_ready = sem("sd_ready")
        pb_ready = sem("pb_ready")
        bt_ready = sem("bt_ready")
        bt_copied = sem("bt_copied")
        bo_ready = sem("bo_ready")
        ao_inv_ready = sem("ao_inv_ready")
        ao_ready = sem("ao_ready")
        aot_ready = sem("aot_ready")
        aot_copied = sem("aot_copied")
        wo_ready = sem("wo_ready")
        var2_ready = sem("var2_ready")
        ve2_ready = sem("ve2_ready")
        rstd2_ready = sem("rstd2_ready")
        x2_ready = sem("x2_ready")
        x2_stored = [sem(f"x2_stored{n}") for n in range(2)]
        x2t_ready = sem("x2t_ready")
        x2t_copied = sem("x2t_copied")
        log_ready = sem("log_ready")
        log_copied = sem("log_copied")
        setup_done = sem("setup_done")
        dve_passed = sem("dve_passed")
        pool_passed = sem("pool_passed")
        pool_setup = sem("pool_setup")
        pinv_ready = sem("pinv_ready")
        r1_ready = sem("r1_ready")
        st1_ready = sem("st1_ready")
        r2_ready = sem("r2_ready")
        st2_ready = sem("st2_ready")

        def pipeline(eng, slot):
            slot(Tile(0, 0), None, None)
            slot(Tile(0, 1), Tile(0, 0), None)
            slot(Tile(1, 0), Tile(0, 1), Tile(0, 0))
            slot(Tile(1, 1), Tile(1, 0), Tile(0, 1))
            with eng.Fori(2, NT // 2) as g:
                slot(Tile(g, 0), Tile(g - 1, 1), Tile(g - 1, 0))
                slot(Tile(g, 1), Tile(g, 0), Tile(g - 1, 1))
            slot(None, Tile(NT // 2 - 1, 1), Tile(NT // 2 - 1, 0))
            slot(None, None, Tile(NT // 2 - 1, 1))

        def expert_pipeline(eng, slot):
            def at(s, back):
                group, place = s[0] + (s[1] - back) // RING, (s[1] - back) % RING
                t = Tile(group, place, RING)
                return None if isinstance(group, int) and not 0 <= t.index < FT else t

            def run(s):
                slot(at(s, 0), at(s, 1), at(s, 2), at(s, 3), at(s, -2))

            ahead = RING + 3
            looped = (FT - 2 - ahead) // RING
            for s in range(ahead):
                run((s // RING, s % RING))
            with eng.Fori(1, 1 + looped) as g:
                for n in range(3, RING + 3):
                    run((g + n // RING, n % RING))
            for s in range(ahead + looped * RING, FT + 3):
                run((s // RING, s % RING))

        block = ctx.enter_context(nc.Block())

        @block.sync
        def _(sp):
            def load_first(a):
                wait_before(sp, s_ready, a, 2)
                wait_before(sp, s_scaled, a, 2)
                wait_before(sp, x1_ready, a, 2)
                at = a.index
                sp.dma_start(xt[a.place][:, :], x_t[:, bass.ts(at, P)]).then_inc(x_in[a.place], 16)
                sp.dma_start(xk[a.place][:, :], x_tok[bass.ts(at, P), :]).then_inc(x_in[a.place], 16)
                for n in range(2):
                    sp.dma_start(scale_bc[a.place][n * S:(n + 1) * S, :],
                                 x_scale[bass.ds(at * 2 + n, 1), :].to_broadcast([S, T])
                                 ).then_inc(x_in[a.place], 16)

            def load_second(a):
                wait_before(sp, kv_ready, a, 2)
                wait_before(sp, sc_masked, a, 2)
                sp.dma_start(ct[a.place][:, :, :].rearrange("p n k -> p (n k)"), ctx_t[:, bass.ts(a.index, 2 * P)]).then_inc(ctx_in[a.place], 16)
                sp.dma_start(mk[a.place][:, :], mask[bass.ts(a.index, P), :]).then_inc(ctx_in[a.place], 16)

            sp.dma_start(kt_sb[:, :], attn_kt).then_inc(consts_in, 16)
            load_first(Tile(0, 0))
            for dst, src in ((cst[:, :], consts), (v_sb[:, :, :], attn_v), (w_qk[:, 0, :], wq), (w_qk[:, 1, :], wk),
                             (w_qk[:, 2, :], wq_swap), (w_qk[:, 3, :], wk_swap), (w_v[:, :], wv), (w_o[:, :], wo),
                             (bo_bc[:, :], bo.to_broadcast([P, D])), (r_w[:, :], router_w),
                             (r_b[:, :], router_b.to_broadcast([P, E]))):
                sp.dma_start(dst, src).then_inc(consts_in, 16)
            load_second(Tile(0, 0))
            load_first(Tile(0, 1))
            load_second(Tile(0, 1))
            with sp.Fori(1, NT // 2) as g:
                for n in range(2):
                    load_first(Tile(g, n))
                    load_second(Tile(g, n))

        CONSTS = 12 * 16
        WEIGHTS = 4 * 16

        @block.tensor
        def _(pe):
            def slot(a, b, c):
                if a:
                    pe.wait_ge(x_in[a.place], (a.group + 1) * 64)
                    wait_before(pe, s_scaled, a)
                    nc.tensor.matmul(ps_s[:, :], xt[a.place][:, :], kt_sb[:, :], start=True,
                                     stop=True).then_inc(s_ready, 1)
                if c:
                    pe.wait_ge(x2_ready, c.done)
                    wait_before(pe, log_copied, c)
                    nc.tensor.transpose(ps_x2t, x2[c.place][:, :], ident).then_inc(x2t_ready, 1)
                if b:
                    pe.wait_ge(ctx_in[b.place], (b.group + 1) * 32)
                    pe.wait_ge(x1_ready, b.done)
                    nc.tensor.transpose(ps_x1t, x1[b.place][:, :], ident).then_inc(x1t_ready, 1)
                    wait_before(pe, ao_ready, b)
                    wait_before(pe, r2_ready, b)
                    nc.tensor.matmul(ps_qk[:, P:2 * P], w_qk[:, 1, :], ct[b.place][:, :, 0:S], start=True, stop=True)
                    nc.tensor.matmul(ps_sw[:, P:2 * P], w_qk[:, 3, :], ct[b.place][:, :, 0:S], start=True, stop=True)
                if c:
                    pe.wait_ge(x2t_copied, c.done)
                    nc.tensor.matmul(ps_log, x2t[:, :], r_w[:, :], start=True, stop=True).then_inc(log_ready, 1)
                if b:
                    pe.wait_ge(x1t_copied, b.done)
                    nc.tensor.matmul(ps_qk[:, 0:P], w_qk[:, 0, :], x1t[:, :], start=True, stop=True)
                    nc.tensor.matmul(ps_sw[:, 0:P], w_qk[:, 2, :], x1t[:, :], start=True,
                                     stop=True).then_inc(q_ready, 1)
                    if c:
                        pe.wait_ge(log_copied, c.done)
                    for n in range(2):
                        mm = nc.tensor.matmul(ps_v[:, n * D:(n + 1) * D], ct[b.place][:, n, :], w_v[:, :], start=True, stop=True)
                    mm.then_inc(kv_ready, 1)
                if a:
                    pe.wait_ge(p_ready, a.done)
                    wait_before(pe, r1_ready, a)
                    for t in range(TB):
                        mm = nc.tensor.transpose(ps_pt[:, t * P:(t + 1) * P], p_sb[:, t * P:(t + 1) * P], ident)
                    mm.then_inc(pt_ready, 1)
                if b:
                    pe.wait_ge(kbd_ready, b.done)
                    pe.wait_ge(v_copied, b.done)
                    for n in range(2):
                        for r in range(RG):
                            rows = slice(r * 32, r * 32 + 32)
                            mm = nc.tensor.matmul(ps_sc[n * S:(n + 1) * S, r, 0:GROUP_KEYS],
                                                  qkt[rows, n * S:(n + 1) * S],
                                                  kbd[rows, n].rearrange("p h k -> p (h k)"),
                                                  start=True, stop=True, tile_position=(r * 32, n * S))
                    mm.then_inc(sc_ready, 1)
                if a:
                    pe.wait_ge(pt_copied, a.done)
                    for t in range(TB):
                        mm = nc.tensor.matmul(ps_o, pt_sb[:, t * P:(t + 1) * P], v_sb[:, t, :], start=(t == 0),
                                              stop=(t == TB - 1))
                    mm.then_inc(o_ready, 1)
                if b:
                    pe.wait_ge(pb_ready, b.done)
                    for h in range(HPAIR):
                        mm = nc.tensor.transpose(ps_bt[:, h * P:(h + 1) * P], pb_sb[:, h * P:(h + 1) * P], ident)
                        if h % (HPAIR // 2) == HPAIR // 2 - 1:
                            mm.then_inc(bt_ready, 1)
                    for h in range(HPAIR):
                        if h % (HPAIR // 2) == 0:
                            pe.wait_ge(bt_copied, b.index * 2 + (1 + h // (HPAIR // 2)))
                        for n in range(2):
                            mm = nc.tensor.matmul(ps_bo[n * S:(n + 1) * S, h * VA:(h + 1) * VA],
                                                  pbt[:, h * P + n * S:h * P + (n + 1) * S],
                                                  vaug[:, n * HPAIR + h, :], start=True, stop=True)
                    mm.then_inc(bo_ready, 1)
                    pe.wait_ge(ao_ready, b.done)
                    nc.tensor.transpose(ps_aot, ao[:, :, :].rearrange("p h d -> p (h d)"), ident).then_inc(aot_ready, 1)
                    pe.wait_ge(aot_copied, b.done)
                    nc.tensor.matmul(ps_wo, aot[:, :], w_o[:, :], start=True, stop=True).then_inc(wo_ready, 1)

            def expert_slot(x, h, y, done, ahead):
                if x:
                    pe.wait_ge(xs_in[x.place], x.landed)
                    wait_before(pe, xst_copied, x)
                    nc.tensor.transpose(ps_xs, xs[x.place][:, :], ident).then_inc(xst_ready, 1)
                if y:
                    pe.wait_ge(h_added, y.done)
                    wait_before(pe, ht_copied, y, 2)
                    for f in range(FB):
                        mm = nc.tensor.transpose(ps_ht[y.place % 2][:, f * P:(f + 1) * P],
                                                 h_sb[y.place % 2][:, f * P:(f + 1) * P], ident)
                    mm.then_inc(ht_ready, 1)
                if h:
                    expert = pe.value_load(expert_of[0:1, bass.ds(h.index, 1)], min_val=0, max_val=E - 1)
                    pe.wait_ge(xst_copied, h.done)
                    wait_before(pe, h_added, h, 2)
                    nc.tensor.matmul(ps_h[h.place % 2], xst[h.place % 2][:, :], w1_sb[:, bass.ts(expert, F)],
                                     start=True, stop=True).then_inc(h_ready, 1)
                if y:
                    expert = pe.value_load(expert_of[0:1, bass.ds(y.index, 1)], min_val=0, max_val=E - 1)
                    pe.wait_ge(ht_copied, y.done)
                    wait_before(pe, yb_ready, y, 2)
                    for f in range(FB):
                        mm = nc.tensor.matmul(ps_y[y.place % 2], ht_sb[y.place % 2][:, f * P:(f + 1) * P],
                                              w2_sb[:, bass.ds(expert * (FB * D) + f * D, D)], start=(f == 0),
                                              stop=(f == FB - 1))
                    mm.then_inc(y_ready, 1)

            pe.wait_ge(consts_in, CONSTS)
            pipeline(pe, slot)

            pe.wait_ge(chosen_ready, 1)
            pe.wait_ge(pool_ones, 1)
            pe.wait_ge(setup_done, 2)
            hot = chosen_bf[:, :, :].rearrange("p t e -> p (t e)")
            nc.tensor.matmul(ps_rank, tri_bf[:, :], hot, start=True, stop=False)
            for t in range(1, NT):
                nc.tensor.matmul(ps_rank[:, t * E:], ones_bf[:, :], hot[:, 0:(NT - t) * E], start=False,
                                 stop=(t == NT - 1))
            for t in range(NT):
                mm = nc.tensor.matmul(ps_count, ones_bf[:, :], hot[:, t * E:(t + 1) * E], start=(t == 0),
                                      stop=(t == NT - 1))
            mm.then_inc(rank_ready, 1)
            pe.wait_ge(hot_ready, 1)
            for t in range(NT):
                mm = nc.tensor.matmul(ps_sorted, lane_hot[:, t, :],
                                      tile_vals[:, t].rearrange("p v j -> p (v j)"), start=(t == 0), stop=(t == NT - 1))
            mm.then_inc(sorted_ready, 1)
            pe.wait_ge(routed, 1)
            pe.wait_ge(weights_in, WEIGHTS)
            expert_pipeline(pe, expert_slot)

        @block.scalar
        def _(act):
            def slot(a, b, c):
                if c:
                    act.wait_ge(x2t_ready, c.done)
                    nc.scalar.copy(x2t[:, :], ps_x2t).then_inc(x2t_copied, 1)
                if b:
                    act.wait_ge(x1t_ready, b.done)
                    nc.scalar.copy(x1t[:, :], ps_x1t).then_inc(x1t_copied, 1)
                if a:
                    act.wait_ge(nmax_ready, a.done)
                    wait_before(act, pt_ready, a)
                    nc.scalar.activation(p_sb[:, :], s_sb[:, :], ACT.Exp, bias=s_nmax[:, :],
                                         accum_out=p_sum[:, :]).then_inc(p_ready, 1)
                    act.wait_ge(pt_ready, a.done)
                    nc.scalar.copy(pt_sb[:, :], ps_pt[:, :]).then_inc(pt_copied, 1)
                if b:
                    act.wait_ge(sd_ready, b.done)
                    nc.scalar.activation(pb_sb[:, :], sd_sb[:, :, :].rearrange("p h k -> p (h k)"),
                                         ACT.Exp).then_inc(pb_ready, 1)
                    for n in range(2):
                        act.wait_ge(bt_ready, b.index * 2 + (1 + n))
                        nc.scalar.copy(pbt[:, n * BANK:(n + 1) * BANK],
                                       ps_bt[:, n * BANK:(n + 1) * BANK]).then_inc(bt_copied, 1)
                    act.wait_ge(aot_ready, b.done)
                    nc.scalar.copy(aot[:, :], ps_aot).then_inc(aot_copied, 1)

            def expert_slot(x, h, y, done, ahead):
                if x:
                    act.wait_ge(xst_ready, x.done)
                    wait_before(act, h_ready, x, 2)
                    nc.scalar.copy(xst[x.place % 2][:, :], ps_xs).then_inc(xst_copied, 1)
                if y:
                    act.wait_ge(ht_ready, y.done)
                    wait_before(act, y_ready, y, 2)
                    nc.scalar.activation(ht_sb[y.place % 2][:, :], ps_ht[y.place % 2],
                                         ACT.Relu).then_inc(ht_copied, 1)

            for dst, src in ((w1_sb, w1), (w2_sb, w2), (b1_bc, b1.to_broadcast([P, E * F])),
                             (b2_bc, b2.to_broadcast([P, E * D]))):
                act.dma_start(dst[:, :], src).then_inc(weights_in, 16)
            pipeline(act, slot)
            act.wait_ge(shifted, 1)
            nc.scalar.activation(lg_exp[:, :, :].rearrange("p t e -> p (t e)"),
                                 lg_sub[:, :, :].rearrange("p t e -> p (t e)"), ACT.Exp).then_inc(exp_ready, 1)
            expert_pipeline(act, expert_slot)

        @block.vector
        def _(dve):
            def norm(r, stats, mv, stats_done, var_ready, rstd, rstd_ready, tile, dst, ready):
                nc.vector.bn_stats(stats[:, :], r[:, :]).then_inc(stats_done, 1)
                dve.wait_ge(stats_done, tile.done)
                carry(dve, dve_passed)
                nc.vector.bn_aggr(mv[:, :], stats[:, :]).then_inc(var_ready, 1)
                dve.wait_ge(rstd_ready, tile.done)
                nc.vector.tensor_scalar(dst, r[:, :], mv[:, 0:1], rstd[:, 0:1], ALU.subtract,
                                        ALU.mult).then_inc(ready, 1)

            def slot(a, b, c):
                if a:
                    dve.wait_ge(s_ready, a.done)
                    dve.wait_ge(x_in[a.place], (a.group + 1) * 64)
                    wait_before(dve, p_ready, a)
                    carry(dve, dve_passed)
                    nc.vector.tensor_tensor_reduce(out=s_sb[:, :], in0=ps_s[:, :], in1=scale_bc[a.place][:, :],
                                                   scale=1.0, scalar=-3.0e38, op0=ALU.mult, op1=ALU.max,
                                                   accum_out=s_max[:, :]).then_inc(s_scaled, 1)
                    dve.wait_ge(s_scaled, a.done)
                    nc.vector.tensor_scalar(s_nmax[:, :], s_max[:, :], -1.0, None, ALU.mult).then_inc(nmax_ready, 1)
                if b:
                    dve.wait_ge(q_ready, b.done)
                    wait_before(dve, qk_ready, b)
                    nc.vector.tensor_tensor(rope_c[:, :], ps_qk, cst[:, C_COS:C_COS + 2 * P], ALU.mult)
                    nc.vector.tensor_tensor(rope_s[:, :], ps_sw, cst[:, C_SIN:C_SIN + 2 * P],
                                            ALU.mult).then_inc(rope_ready, 1)
                if c:
                    dve.wait_ge(log_ready, c.done)
                    nc.vector.tensor_tensor(logits[:, bass.ds(c.index, 1), :].rearrange("p t e -> p (t e)"), ps_log,
                                            r_b[:, :], ALU.add).then_inc(log_copied, 1)
                if b:
                    dve.wait_ge(kv_ready, b.done)
                    wait_before(dve, bo_ready, b)
                    for n in range(2):
                        rows = slice(n * S, (n + 1) * S)
                        cp = nc.vector.tensor_copy(vaug[rows, :, n * (HD + 1):n * (HD + 1) + HD],
                                                   ps_v[rows, :].rearrange("p (g h d) -> p g h d", h=2, d=HD)[:, :, n, :])
                    cp.then_inc(v_copied, 1)
                    dve.wait_ge(sc_ready, b.done)
                    dve.wait_ge(sc_filled, b.done)
                    dve.wait_ge(ctx_in[b.place], (b.group + 1) * 32)
                    keep = mk[b.place][:, :].unsqueeze(1).unsqueeze(1).to_broadcast([P, RG, HG, S])
                    carry(dve, dve_passed)
                    nc.vector.copy_predicated(sc_sb[:, :, :].rearrange("p (r h) k -> p r h k", r=RG), keep,
                                              sc_view.rearrange("p r (h k) -> p r h k", k=S)).then_inc(sc_masked, 1)
                    dve.wait_ge(sc_masked, b.done)
                    nc.vector.tensor_reduce(sc_max[:, :], sc_sb[:, :, :], AX.X, ALU.max).then_inc(scmax_ready, 1)
                if a:
                    dve.wait_ge(p_ready, a.done)
                    nc.vector.reciprocal(p_inv[:, :], p_sum[:, :]).then_inc(pinv_ready, 1)
                    dve.wait_ge(pinv_ready, a.done)
                    dve.wait_ge(o_ready, a.done)
                    nc.vector.scalar_tensor_tensor(out=r1[:, :], in0=ps_o, scalar=p_inv[:, 0:1],
                                                   in1=xk[a.place][:, :], op0=ALU.mult, op1=ALU.add).then_inc(r1_ready, 1)
                    dve.wait_ge(r1_ready, a.done)
                    wait_before(dve, wo_ready, a, 2)
                    wait_before(dve, x1b_ready, a, 2)
                    norm(r1, st1, mv1, st1_ready, var1_ready, rstd1, rstd1_ready, a, x1[a.place][:, :], x1_ready)
                if b:
                    dve.wait_ge(bo_ready, b.done)
                    bo_view = ps_bo.rearrange("p (h c) -> p h c", c=HD + 1)
                    nc.vector.reciprocal(ao_inv[:, :], bo_view[:, :, HD:HD + 1].rearrange("p h c -> p (h c)")
                                         ).then_inc(ao_inv_ready, 1)
                    dve.wait_ge(ao_inv_ready, b.done)
                    nc.vector.tensor_tensor(ao[:, :, :], bo_view[:, :, 0:HD],
                                            spread(ao_inv[:, :], 2, [P, HEADS, HD]), ALU.mult).then_inc(ao_ready, 1)
                    dve.wait_ge(wo_ready, b.done)
                    dve.wait_ge(x1b_ready, b.done)
                    nc.vector.tensor_tensor(r2[:, :], ps_wo, x1b[:, :], ALU.add).then_inc(r2_ready, 1)
                    dve.wait_ge(r2_ready, b.done)
                    if not (isinstance(b.group, int) and b.group == 0):
                        dve.wait_ge(x2_stored[b.place], b.group * 16)
                    wait_before(dve, x2t_ready, b, 2)
                    norm(r2, st2, mv2, st2_ready, var2_ready, rstd2, rstd2_ready, b, x2[b.place][:, :], x2_ready)

            def routing():
                steps = [0]

                def then(ins):
                    steps[0] += 1
                    ins.then_inc(route, 1)
                    dve.wait_ge(route, steps[0])

                v = nc.vector
                dve.wait_ge(log_copied, NT)
                then(v.tensor_reduce(lg_max[:, :], logits[:, :, :], AX.X, ALU.max))
                v.tensor_tensor(lg_sub[:, :, :], logits[:, :, :], spread(lg_max[:, :], 2, [P, NT, E]),
                                ALU.subtract).then_inc(shifted, 1)
                then(v.tensor_tensor(at_max[:, :, :], logits[:, :, :], spread(lg_max[:, :], 2, [P, NT, E]),
                                     ALU.is_ge))
                weight8 = spread(cst[:, C_W8:C_W8 + E], 1, [P, NT, E])
                then(v.tensor_tensor(chosen[:, :, :], at_max[:, :, :], weight8, ALU.mult))
                then(v.tensor_reduce(first[:, :], chosen[:, :, :], AX.X, ALU.max))
                then(v.tensor_tensor(chosen[:, :, :], weight8, spread(first[:, :], 2, [P, NT, E]), ALU.is_equal))
                v.tensor_copy(chosen_bf[:, :, :], chosen[:, :, :]).then_inc(chosen_ready, 1)
                dve.wait_ge(exp_ready, 1)
                then(v.tensor_reduce(first[:, :], lg_exp[:, :, :], AX.X, ALU.add))
                then(v.reciprocal(gate[:, :], first[:, :]))
                then(v.tensor_copy(vals[:, :, 0:2],
                                   cst[:, C_TOK:C_TOK + 2 * NT].rearrange("p (t v) -> p t v", v=2)))
                then(v.tensor_copy(vals[:, :, 2], gate[:, :]))
                then(v.tensor_tensor(gate_rest[:, :], gate[:, :], vals[:, :, 2], ALU.subtract))
                then(v.tensor_copy(vals[:, :, 3], gate_rest[:, :]))
                then(v.tensor_tensor(gate[:, :], gate_rest[:, :], vals[:, :, 3], ALU.subtract))
                then(v.tensor_copy(vals[:, :, 4], gate[:, :]))
                dve.wait_ge(rank_ready, 1)
                then(v.tensor_scalar(whole[:, :], ps_count, float(P - 1), None, ALU.add))
                then(v.tensor_copy(whole_i[:, :], whole[:, :]))
                then(v.tensor_scalar(whole_i[:, :], whole_i[:, :], 7, None, ALU.arith_shift_right))
                then(v.tensor_copy(whole[:, :], whole_i[:, :]))
                then(v.tensor_copy(ends[:, 0:1], whole[:, 0:1]))
                for e in range(1, E):
                    then(v.tensor_tensor(ends[:, e:e + 1], ends[:, e - 1:e], whole[:, e:e + 1], ALU.add))
                then(v.tensor_tensor(starts[:, :], ends[:, :], whole[:, :], ALU.subtract))
                then(v.tensor_scalar(starts[:, :], starts[:, :], float(P), None, ALU.mult))
                then(v.tensor_tensor(place_e[:, :, :], ps_rank.rearrange("p (t e) -> p t e", e=E),
                                     spread(starts[:, :], 1, [P, NT, E]), ALU.add))
                then(v.tensor_tensor(place_e[:, :, :], place_e[:, :, :], chosen[:, :, :], ALU.mult))
                then(v.tensor_reduce(place_f[:, :], place_e[:, :, :], AX.X, ALU.add))
                then(v.tensor_copy(place_i[:, :], place_f[:, :]))
                then(v.tensor_scalar(part_i[:, :], place_i[:, :], P - 1, None, ALU.bitwise_and))
                then(v.tensor_copy(lane_f[:, :], part_i[:, :]))
                then(v.tensor_scalar(part_i[:, :], place_i[:, :], 7, None, ALU.arith_shift_right))
                then(v.tensor_copy(tile_f[:, :], part_i[:, :]))
                then(v.tensor_tensor(tile_hot[:, :, :], spread(cst[:, C_IOTA:C_IOTA + FT], 1, [P, NT, FT]),
                                     spread(tile_f[:, :], 2, [P, NT, FT]), ALU.is_equal))
                then(v.tensor_tensor(tile_vals[:, :, :, :], spread(tile_hot[:, :, :], 2, [P, NT, VALS, FT]),
                                     spread(vals[:, :, :], 3, [P, NT, VALS, FT]), ALU.mult))
                v.tensor_tensor(lane_hot[:, :, :], spread(cst[:, C_IOTA:C_IOTA + P], 1, [P, NT, P]),
                                spread(lane_f[:, :], 2, [P, NT, P]), ALU.is_equal).then_inc(hot_ready, 1)
                then(v.tensor_tensor(past[:, :, :], spread(cst[:, C_IOTA:C_IOTA + FT], 2, [P, FT, E]),
                                     spread(ends[:, :], 1, [P, FT, E]), ALU.is_ge))
                then(v.tensor_reduce(expert_f[:, :], past[:, :, :], AX.X, ALU.add))
                then(v.tensor_scalar(expert_low[:, :], expert_f[:, :], float(E - 1), None, ALU.min))
                then(v.tensor_copy(expert_of[:, :], expert_low[:, :]))
                dve.wait_ge(sorted_ready, 1)
                then(v.tensor_copy(sorted_sb[:, :, :].rearrange("p v j -> p (v j)"), ps_sorted))
                then(v.scalar_tensor_tensor(out=row_f[:, :], in0=sorted_sb[:, 0, :], scalar=float(P),
                                            in1=sorted_sb[:, 1, :], op0=ALU.mult, op1=ALU.add))
                then(v.tensor_scalar(from_f[:, :], row_f[:, :], -float(P), 0.0, ALU.add, ALU.max))
                then(v.tensor_copy(from_row[:, :], from_f[:, :]))
                then(v.tensor_scalar(to_f[:, :], sorted_sb[:, 0, :], 0.5, float(2 * NT * P), ALU.is_lt, ALU.mult))
                then(v.tensor_tensor(to_f[:, :], to_f[:, :], from_f[:, :], ALU.add))
                then(v.tensor_copy(to_row[:, :], to_f[:, :]))
                then(v.tensor_tensor(gate_sum[:, :], sorted_sb[:, 3, :], sorted_sb[:, 4, :], ALU.add))
                v.tensor_tensor(sorted_gate[:, :], sorted_sb[:, 2, :], gate_sum[:, :], ALU.add).then_inc(routed, 1)
                dve.wait_ge(routed, 1)

            def expert_slot(x, h, y, done, ahead):
                if h:
                    expert = dve.value_load(expert_of[0:1, bass.ds(h.index, 1)], min_val=0, max_val=E - 1)
                    dve.wait_ge(h_ready, h.done)
                    wait_before(dve, ht_ready, h, 2)
                    nc.vector.tensor_tensor(h_sb[h.place % 2][:, :], ps_h[h.place % 2],
                                            b1_bc[:, bass.ts(expert, F)], ALU.add).then_inc(h_added, 1)
                if y:
                    expert = dve.value_load(expert_of[0:1, bass.ds(y.index, 1)], min_val=0, max_val=E - 1)
                    dve.wait_ge(y_ready, y.done)
                    wait_before(dve, r3_ready, y)
                    nc.vector.tensor_tensor(yb[:, :], ps_y[y.place % 2], b2_bc[:, bass.ts(expert, D)],
                                            ALU.add).then_inc(yb_ready, 1)
                if done:
                    dve.wait_ge(rstd3_ready, done.done)
                    if not (isinstance(done.group, int) and done.group == 0):
                        dve.wait_ge(out_stored[done.place], done.group * 16)
                    nc.vector.tensor_scalar(res[done.place][:, :], r3[done.place % 2][:, :],
                                            mv3[done.place % 2][:, 0:1], rstd3[done.place % 2][:, 0:1], ALU.subtract,
                                            ALU.mult).then_inc(res_ready, 1)
                if y:
                    dve.wait_ge(yb_ready, y.done)
                    wait_before(dve, res_ready, y, 2)
                    nc.vector.scalar_tensor_tensor(out=r3[y.place % 2][:, :], in0=yb[:, :],
                                                   scalar=sorted_gate[:, bass.ds(y.index, 1)], in1=xs[y.place][:, :],
                                                   op0=ALU.mult, op1=ALU.add).then_inc(r3_ready, 1)
                    dve.wait_ge(r3_ready, y.done)
                    nc.vector.bn_stats(st3[:, :], r3[y.place % 2][:, :]).then_inc(st3_ready, 1)
                    dve.wait_ge(st3_ready, y.done)
                    carry(dve, dve_passed)
                    nc.vector.bn_aggr(mv3[y.place % 2][:, :], st3[:, :]).then_inc(var3_ready, 1)

            dve.wait_ge(consts_in, CONSTS)
            nc.vector.tensor_copy(vaug[:, :, :].rearrange("p g c -> p (g c)"),
                                  cst[:, C_VA:C_VA + 2 * HPAIR * VA]).then_inc(setup_done, 1)
            nc.vector.tensor_copy(tri_bf[:, :], cst[:, C_TRI:C_TRI + P]).then_inc(setup_done, 1)
            dve.wait_ge(setup_done, 2)
            pipeline(dve, slot)
            routing()
            dve.wait_ge(weights_in, WEIGHTS)
            expert_pipeline(dve, expert_slot)

        @block.gpsimd
        def _(pool):
            def root(var, ve, ready_var, ve_ready, rstd, rstd_ready, tile):
                pool.wait_ge(ready_var, tile.done)
                carry(pool, pool_passed)
                nc.gpsimd.tensor_scalar(ve[:, :], var, EPS, 1.0, ALU.add, ALU.mult).then_inc(ve_ready, 1)
                pool.wait_ge(ve_ready, tile.done)
                nc.gpsimd.tensor_tensor(rstd[:, :], ve[:, :], half_neg[:, :], ALU.pow).then_inc(rstd_ready, 1)

            def slot(a, b, c):
                if b:
                    wait_before(pool, sd_ready, b)
                    carry(pool, pool_passed)
                    nc.gpsimd.memset(sc_sb[:, :, :], MASKED).then_inc(sc_filled, 1)
                    pool.wait_ge(x1_ready, b.done)
                    wait_before(pool, r2_ready, b)
                    nc.gpsimd.tensor_tensor(x1b[:, :], x1[b.place][:, :], bo_bc[:, :], ALU.add).then_inc(x1b_ready, 1)
                    pool.wait_ge(rope_ready, b.done)
                    wait_before(pool, sc_ready, b)
                    nc.gpsimd.tensor_tensor(qkt[:, :], rope_c[:, :], rope_s[:, :], ALU.add).then_inc(qk_ready, 1)
                    pool.wait_ge(qk_ready, b.done)
                    for n in range(2):
                        mm = nc.gpsimd.tensor_tensor(
                            kbd[:, n], spread(qkt[:, P + n * S:P + (n + 1) * S], 1, [P, HG, S]),
                            spread(cst[:, C_HM:C_HM + HG], 2, [P, HG, S]), ALU.mult)
                    mm.then_inc(kbd_ready, 1)
                    pool.wait_ge(scmax_ready, b.done)
                    wait_before(pool, pb_ready, b)
                    nc.gpsimd.tensor_tensor(sd_sb[:, :, :], sc_sb[:, :, :], spread(sc_max[:, :], 2, [P, HEADS, S]),
                                            ALU.subtract).then_inc(sd_ready, 1)
                if a:
                    root(mv1[:, 1:2], ve1, var1_ready, ve1_ready, rstd1, rstd1_ready, a)
                if b:
                    root(mv2[:, 1:2], ve2, var2_ready, ve2_ready, rstd2, rstd2_ready, b)
                    pool.wait_ge(x2_ready, b.done)
                    pool.dma_start(x2_dram[bass.ts(b.index, P), :], x2[b.place][:, :]).then_inc(x2_stored[b.place], 16)

            def gather(j):
                wait_before(pool, r3_ready, j, RING)
                nc.gpsimd.tensor_copy(from_cur[j.place][:, :], from_row[:, bass.ds(j.index, 1)]
                                      ).then_inc(from_copied, 1)
                pool.wait_ge(from_copied, j.done)
                carry(pool, pool_passed)
                pool.indirect_dma_start(xs[j.place][:, :], None, x2_dram,
                                        bass.IndirectOffsetOnAxis(from_cur[j.place][:, :], 0)
                                        ).then_inc(xs_in[j.place], 16)

            def expert_slot(x, h, y, done, ahead):
                if y:
                    root(mv3[y.place % 2][:, 1:2], ve3, var3_ready, ve3_ready, rstd3[y.place % 2], rstd3_ready, y)
                if ahead and not (isinstance(ahead.index, int) and ahead.index < RING):
                    gather(ahead)
                if done:
                    if not (isinstance(done.group, int) and done.group == 0):
                        pool.wait_ge(out_stored[done.place], done.group * 16)
                    nc.gpsimd.tensor_copy(to_cur[done.place][:, :], to_row[:, bass.ds(done.index, 1)]
                                          ).then_inc(to_copied, 1)
                    pool.wait_ge(to_copied, done.done)
                    pool.wait_ge(res_ready, done.done)
                    carry(pool, pool_passed)
                    pool.indirect_dma_start(out, bass.IndirectOffsetOnAxis(to_cur[done.place][:, :], 0),
                                            res[done.place][:, :], None, bounds_check=NT * P - 1, oob_is_err=False
                                            ).then_inc(out_stored[done.place], 16)

            nc.gpsimd.memset(ones_bf[:, :], 1.0).then_inc(pool_ones, 1)
            nc.gpsimd.memset(half_neg[:, :], -0.5).then_inc(pool_setup, 1)
            pool.wait_ge(pool_setup, 1)
            pool.wait_ge(consts_in, CONSTS)
            pipeline(pool, slot)
            pool.wait_ge(routed, 1)
            for n in range(2):
                pool.wait_ge(x2_stored[n], NT // 2 * 16)
            for n in range(RING):
                gather(Tile(0, n, RING))
            expert_pipeline(pool, expert_slot)
            for n in range(RING):
                pool.wait_ge(out_stored[n], len(range(n, FT, RING)) * 16)


_IN = ["x_tok", "x_t", "x_scale", "ctx_t", "mask", "attn_kt", "attn_v", "wq", "wq_swap", "wk", "wk_swap", "wv", "wo",
       "bo", "router_w", "router_b", "w1", "b1", "w2", "b2", "consts"]


def _constants():
    import numpy as np

    c = np.zeros((P, C_ALL), np.float32)
    c[:, C_ID:C_ID + P] = np.eye(P)
    inv_freq = (1.0 / np.float32(10000.0) ** (np.arange(0, HD, 2, dtype=np.float32) / np.float32(HD))).astype(np.float32)
    angle = (np.arange(S, dtype=np.float32)[:, None] * inv_freq[None, :]).astype(np.float32)
    feature = np.arange(P)
    pair = (feature % HD) // 2
    cos, sin = np.cos(angle)[:, pair].T, np.sin(angle)[:, pair].T
    sin = sin * np.where(feature % 2 == 0, -1.0, 1.0)[:, None]
    root = np.float32(1.0 / np.sqrt(HD))
    for n in range(2):
        c[:, C_COS + n * S:C_COS + (n + 1) * S] = cos * root
        c[:, C_COS + P + n * S:C_COS + P + (n + 1) * S] = cos
        c[:, C_SIN + n * S:C_SIN + (n + 1) * S] = sin * root
        c[:, C_SIN + P + n * S:C_SIN + P + (n + 1) * S] = sin
    c[feature, C_HM + (feature // HD) % HG] = 1.0
    va = np.zeros((P, 2 * HPAIR, VA), np.float32)
    va[:S, :, HD] = 1.0
    va[S:, :, 2 * HD + 1] = 1.0
    c[:, C_VA:C_VA + 2 * HPAIR * VA] = va.reshape(P, -1)
    c[:, C_TRI:C_TRI + P] = feature[:, None] < feature[None, :]
    c[:, C_IOTA:C_IOTA + P] = feature[None, :]
    c[:, C_W8:C_W8 + E] = E - np.arange(E)[None, :]
    tok = np.zeros((P, NT, 2), np.float32)
    tok[:, :, 0] = np.arange(NT)[None, :] + 1
    tok[:, :, 1] = feature[:, None]
    c[:, C_TOK:C_TOK + 2 * NT] = tok.reshape(P, -1)
    return c


def kernel(**inputs):
    import numpy as np
    import concourse.bacc as bacc
    from concourse.bass_utils import run_bass_kernel_spmd

    i = {k: np.asarray(v) for k, v in inputs.items()}
    x = i["x"].reshape(NT * P, D)
    swap = np.arange(D) ^ 1
    arrays = {
        "x_tok": x,
        "x_t": x.T,
        "x_scale": i["x"][:, ::S // 4, :].reshape(B, T),
        "ctx_t": np.repeat(i["ctx_1024"][:, None], 2, axis=1).reshape(2 * NT * P, D).T,
        "mask": i["mask_Bx1xSxS2_ik1"].reshape(NT * P, S),
        "attn_kt": i["L0_attn_k"][0].T,
        "attn_v": i["L0_attn_v"][0].reshape(TB, P, D).transpose(1, 0, 2),
        "wq": i["L0_xattn_Wq"], "wq_swap": i["L0_xattn_Wq"][:, swap],
        "wk": i["L0_xattn_Wk"], "wk_swap": i["L0_xattn_Wk"][:, swap],
        "wv": i["L0_xattn_Wv"], "wo": i["L0_xattn_Wo"], "bo": i["L0_xattn_bo"].reshape(1, D),
        "router_w": i["L0_ffn_router_W"], "router_b": i["L0_ffn_router_b"].reshape(1, E),
        "w1": i["L0_ffn_W1"].transpose(1, 0, 2).reshape(P, E * F),
        "b1": i["L0_ffn_b1"].reshape(1, E * F),
        "w2": i["L0_ffn_W2"].reshape(E, FB, P, D).transpose(2, 0, 1, 3).reshape(P, E * FB * D),
        "b2": i["L0_ffn_b2"].reshape(1, E * D),
        "consts": _constants(),
    }
    nc = bacc.Bacc("TRN2", target_bir_lowering=False, num_devices=1)
    feeds, args = {}, []
    for name in _IN:
        a = np.ascontiguousarray(arrays[name])
        feeds[f"in_{name}"] = a
        args.append(nc.dram_tensor(f"in_{name}", a.shape, mybir.dt.from_np(a.dtype), kind="ExternalInput").ap())
    result = nc.dram_tensor("out", (NT * P, D), F32, kind="ExternalOutput").ap()
    decoder_kernel(nc, *args, result)
    r = run_bass_kernel_spmd(nc, [feeds], core_ids=[0])
    return np.asarray(r.results[0]["out"]).reshape(B, S, D)
```

```python
from contextlib import ExitStack

import concourse.bass as bass
from concourse import mybir

ALU = mybir.AluOpType
ACT = mybir.ActivationFunctionType
AX = mybir.AxisListType
F32 = mybir.dt.float32
BF16 = mybir.dt.bfloat16
I32 = mybir.dt.int32
U32 = mybir.dt.uint32

P = 128
B, S, D = 32, 64, 128
NT = B * S // P
T = 512
TB = T // P
HEADS, HD = 16, 8
HPAIR = HEADS // 2
RG = 4
HG = HEADS // RG
GROUP_KEYS = HG * S
BANK = 512
VA = 2 * (HD + 1)
E, F = 8, 512
FB = F // P
FT = NT + E - 1
RING = 4
VALS = 5
EPS = 1e-5
MASKED = -10000.0

C_ID = 0
C_COS = C_ID + P
C_SIN = C_COS + 2 * P
C_HM = C_SIN + 2 * P
C_VA = C_HM + HG
C_TRI = C_VA + 2 * HPAIR * VA
C_IOTA = C_TRI + P
C_W8 = C_IOTA + P
C_TOK = C_W8 + E
C_ALL = C_TOK + 2 * NT


class Tile:

    def __init__(self, group, place, per=2):
        self.group, self.place, self.per = group, place, per

    @property
    def index(self):
        return self.group * self.per + self.place

    @property
    def done(self):
        return self.index + 1

    @property
    def landed(self):
        return (self.group + 1) * 16


def wait_before(eng, sem, tile, back=1):
    if isinstance(tile.index, int) and tile.index < back:
        return
    eng.wait_ge(sem, tile.index + (1 - back))


def carry(eng, passed):
    eng.sem_inc(passed, 1)


def spread(ap, axis, shape):
    return ap.unsqueeze(axis).to_broadcast(shape)


def decoder_kernel(nc, x_tok, x_t, x_scale, ctx_t, mask, attn_kt, attn_v, wq, wq_swap, wk, wk_swap, wv, wo, bo,
                   router_w, router_b, w1, b1, w2, b2, consts, out):
    with ExitStack() as ctx:
        def sb(name, shape, dt=F32):
            return ctx.enter_context(nc.sbuf_tensor(name, shape, dt))

        def psum(name, shape, dt=F32):
            return ctx.enter_context(nc.psum_tensor(name, shape, dt))

        def sem(name):
            return ctx.enter_context(nc.semaphore(name))

        x2_dram = nc.dram_tensor("x2_rows", [NT * P, D], F32, kind="Internal").ap()

        cst = sb("cst", [P, C_ALL])
        ident = cst[:, C_ID:C_ID + P]
        kt_sb = sb("kt_sb", [P, T])
        v_sb = sb("v_sb", [P, TB, D])
        w_qk = sb("w_qk", [P, 4, D])
        w_v = sb("w_v", [P, D])
        w_o = sb("w_o", [P, D])
        bo_bc = sb("bo_bc", [P, D])
        r_w = sb("r_w", [P, E])
        r_b = sb("r_b", [P, E])

        xt = [sb(f"xt{n}", [P, P]) for n in range(2)]
        xk = [sb(f"xk{n}", [P, D]) for n in range(2)]
        scale_bc = [sb(f"scale_bc{n}", [P, T]) for n in range(2)]
        s_sb = sb("s_sb", [P, T])
        s_max = sb("s_max", [P, 1])
        s_nmax = sb("s_nmax", [P, 1])
        p_sb = sb("p_sb", [P, T])
        p_sum = sb("p_sum", [P, 1])
        p_inv = sb("p_inv", [P, 1])
        pt_sb = sb("pt_sb", [P, T])
        r1 = sb("r1", [P, D])
        st1 = sb("st1", [P, 6])
        mv1 = sb("mv1", [P, 2])
        rstd1 = sb("rstd1", [P, 1])
        x1 = [sb(f"x1_{n}", [P, D]) for n in range(2)]

        ct = [sb(f"ct{n}", [P, 2, P]) for n in range(2)]
        mk = [sb(f"mk{n}", [P, S], I32) for n in range(2)]
        x1b = sb("x1b", [P, NT * D])
        x1t = sb("x1t", [P, P])
        rope_c = sb("rope_c", [P, 2 * P])
        rope_s = sb("rope_s", [P, 2 * P])
        qkt = [sb(f"qkt{n}", [P, 2 * P]) for n in range(2)]
        kbd = [sb(f"kbd{n}", [P, 2, HG, S]) for n in range(2)]
        vaug = [sb(f"vaug{n}", [P, HPAIR, 2, VA]) for n in range(2)]
        sc_sb = sb("sc_sb", [P, HEADS, S])
        sc_max = sb("sc_max", [P, HEADS])
        sd_sb = sb("sd_sb", [P, HEADS, S])
        pb_sb = [sb(f"pb_sb{n}", [P, HEADS * S]) for n in range(2)]
        pbt = sb("pbt", [P, HEADS * S])
        ao_inv = sb("ao_inv", [P, HEADS])
        ao = sb("ao", [P, HEADS, HD])
        aot = sb("aot", [P, P])
        r2 = sb("r2", [P, D])
        st2 = sb("st2", [P, 6])
        mv2 = sb("mv2", [P, 2])
        rstd2 = sb("rstd2", [P, 1])
        x2 = [sb(f"x2_{n}", [P, D]) for n in range(2)]
        x2t = sb("x2t", [P, P])
        logits = sb("logits", [P, NT, E])
        half_neg = sb("half_neg", [P, 1])
        ve1 = sb("ve1", [P, 1])
        ve2 = sb("ve2", [P, 1])

        tri_bf = sb("tri_bf", [P, P], BF16)
        ones_bf = sb("ones_bf", [P, P], BF16)
        lg_max = sb("lg_max", [P, NT])
        lg_exp = sb("lg_exp", [P, NT, E])
        lg_sub = sb("lg_sub", [P, NT, E])
        gate = sb("gate", [P, NT])
        gate_rest = sb("gate_rest", [P, NT])
        at_max = sb("at_max", [P, NT, E])
        first = sb("first", [P, NT])
        chosen = sb("chosen", [P, NT, E])
        chosen_bf = sb("chosen_bf", [P, NT, E], BF16)
        whole = sb("whole", [P, E])
        whole_i = sb("whole_i", [P, E], I32)
        ends = sb("ends", [P, E])
        starts = sb("starts", [P, E])
        place_e = sb("place_e", [P, NT, E])
        place_f = sb("place_f", [P, NT])
        place_i = sb("place_i", [P, NT], I32)
        part_i = sb("part_i", [P, NT], I32)
        lane_f = sb("lane_f", [P, NT])
        tile_f = sb("tile_f", [P, NT])
        lane_hot = sb("lane_hot", [P, NT, P], BF16)
        tile_hot = sb("tile_hot", [P, NT, FT], BF16)
        vals = sb("vals", [P, NT, VALS], BF16)
        tile_vals = sb("tile_vals", [P, NT, VALS, FT], BF16)
        sorted_sb = sb("sorted_sb", [P, VALS, FT])
        row_f = sb("row_f", [P, FT])
        from_f = sb("from_f", [P, FT])
        to_f = sb("to_f", [P, FT])
        from_row = sb("from_row", [P, FT], U32)
        to_row = sb("to_row", [P, FT], U32)
        gate_sum = sb("gate_sum", [P, FT])
        sorted_gate = sb("sorted_gate", [P, FT])
        past = sb("past", [P, FT, E])
        expert_f = sb("expert_f", [P, FT])
        expert_low = sb("expert_low", [P, FT])
        expert_of = sb("expert_of", [P, FT], I32)

        w1_sb = sb("w1_sb", [P, E * F])
        w2_sb = sb("w2_sb", [P, E * FB * D])
        b1_bc = sb("b1_bc", [P, E * F])
        b2_bc = sb("b2_bc", [P, E * D])
        from_cur = [sb(f"from_cur{n}", [P, 1], U32) for n in range(RING)]
        to_cur = [sb(f"to_cur{n}", [P, 1], U32) for n in range(RING)]
        xs = [sb(f"xs{n}", [P, D]) for n in range(RING)]
        xst = [sb(f"xst{n}", [P, P]) for n in range(2)]
        h_sb = [sb(f"h_sb{n}", [P, F]) for n in range(2)]
        ht_sb = [sb(f"ht_sb{n}", [P, F]) for n in range(2)]
        yb = sb("yb", [P, D])
        r3 = [sb(f"r3_{n}", [P, D]) for n in range(2)]
        st3 = sb("st3", [P, 6])
        mv3 = [sb(f"mv3_{n}", [P, 2]) for n in range(2)]
        ve3 = sb("ve3", [P, 1])
        rstd3 = [sb(f"rstd3_{n}", [P, 1]) for n in range(2)]
        res = [sb(f"res{n}", [P, D]) for n in range(RING)]

        ps_s = psum("ps_s", [P, BANK])
        ps_pt = psum("ps_pt", [P, BANK])
        ps_o = ps_pt[:, 0:D]
        ps_p = psum("ps_p", [P, BANK])
        ps_x1t = ps_p[:, 0:P]
        ps_x2t = ps_p[:, P:2 * P]
        ps_sc = psum("ps_sc", [P, 2 * BANK])
        ps_bt = psum("ps_bt", [P, 2 * BANK])
        ps_bo = ps_bt[:, 0:HPAIR * 2 * VA]
        ps_aot = ps_bt[:, 0:P]
        ps_wo = ps_bt[:, P:P + D]
        ps_vl = psum("ps_vl", [P, BANK])
        ps_log = ps_vl[:, 2 * D:2 * D + E]
        ps_v = ps_vl[:, 0:2 * D]
        ps_rank = ps_p[:, 0:NT * E]
        ps_count = ps_s[:, 0:E]
        ps_sorted = ps_pt[:, 0:VALS * FT]
        ps_h = [ps_s[:, :], ps_pt[:, :]]
        ps_ht = [ps_bt[:, 0:F], ps_bt[:, F:2 * F]]
        ps_xs = ps_p[:, 0:P]
        ps_y = [ps_sc[:, 0:D], ps_sc[:, BANK:BANK + D]]

        consts_in = sem("consts_in")
        keys_in = sem("keys_in")
        proj_in = sem("proj_in")
        weights_in = sem("weights_in")
        pool_ones = sem("pool_ones")
        route = sem("route")
        shifted = sem("shifted")
        exp_ready = sem("exp_ready")
        chosen_ready = sem("chosen_ready")
        rank_ready = sem("rank_ready")
        hot_ready = sem("hot_ready")
        sorted_ready = sem("sorted_ready")
        routed = sem("routed")
        xs_in = [sem(f"xs_in{n}") for n in range(RING)]
        from_copied = sem("from_copied")
        to_copied = sem("to_copied")
        xst_ready = sem("xst_ready")
        xst_copied = sem("xst_copied")
        h_ready = sem("h_ready")
        h_added = sem("h_added")
        ht_ready = sem("ht_ready")
        ht_copied = sem("ht_copied")
        y_ready = sem("y_ready")
        yb_ready = sem("yb_ready")
        r3_ready = sem("r3_ready")
        st3_ready = sem("st3_ready")
        var3_ready = sem("var3_ready")
        ve3_ready = sem("ve3_ready")
        rstd3_ready = sem("rstd3_ready")
        res_ready = sem("res_ready")
        out_stored = [sem(f"out_stored{n}") for n in range(RING)]
        x_in = [sem(f"x_in{n}") for n in range(2)]
        ctx_in = [sem(f"ctx_in{n}") for n in range(2)]
        s_ready = sem("s_ready")
        s_scaled = sem("s_scaled")
        nmax_ready = sem("nmax_ready")
        p_ready = sem("p_ready")
        pt_ready = sem("pt_ready")
        pt_copied = sem("pt_copied")
        o_ready = sem("o_ready")
        var1_ready = sem("var1_ready")
        ve1_ready = sem("ve1_ready")
        rstd1_ready = sem("rstd1_ready")
        x1_ready = sem("x1_ready")
        x1b_ready = sem("x1b_ready")
        x1t_ready = sem("x1t_ready")
        x1t_copied = sem("x1t_copied")
        v_ready = sem("v_ready")
        q_ready = sem("q_ready")
        v_copied = sem("v_copied")
        rope_ready = sem("rope_ready")
        qk_ready = sem("qk_ready")
        kbd_ready = sem("kbd_ready")
        sc_filled = sem("sc_filled")
        sc_half = sem("sc_half")
        sc_ready = sem("sc_ready")
        sc_masked = sem("sc_masked")
        scmax_ready = sem("scmax_ready")
        sd_ready = sem("sd_ready")
        pb_ready = sem("pb_ready")
        bt_ready = sem("bt_ready")
        bt_copied = sem("bt_copied")
        bo_ready = sem("bo_ready")
        ao_inv_ready = sem("ao_inv_ready")
        ao_ready = sem("ao_ready")
        aot_ready = sem("aot_ready")
        aot_copied = sem("aot_copied")
        wo_ready = sem("wo_ready")
        var2_ready = sem("var2_ready")
        ve2_ready = sem("ve2_ready")
        rstd2_ready = sem("rstd2_ready")
        x2_ready = sem("x2_ready")
        x2_stored = [sem(f"x2_stored{n}") for n in range(2)]
        x2t_ready = sem("x2t_ready")
        x2t_copied = sem("x2t_copied")
        log_ready = sem("log_ready")
        log_copied = sem("log_copied")
        setup_done = sem("setup_done")
        dve_passed = sem("dve_passed")
        pool_passed = sem("pool_passed")
        pool_setup = sem("pool_setup")
        pinv_ready = sem("pinv_ready")
        r1_ready = sem("r1_ready")
        st1_ready = sem("st1_ready")
        r2_ready = sem("r2_ready")
        st2_ready = sem("st2_ready")

        STAGES = 6

        def pipeline(eng, slot, looped=NT // 2):
            def run(group, place):
                def at(back):
                    t = Tile(group + (place - back) // 2, (place - back) % 2)
                    return None if isinstance(group, int) and not 0 <= t.index < NT else t
                slot(*(at(back) for back in range(STAGES)))

            for s in range(STAGES):
                run(s // 2, s % 2)
            with eng.Fori(STAGES // 2, looped) as g:
                run(g, 0)
                run(g, 1)
            for s in range(2 * looped, NT + STAGES - 1):
                run(s // 2, s % 2)

        def expert_pipeline(eng, slot):
            def at(s, back):
                group, place = s[0] + (s[1] - back) // RING, (s[1] - back) % RING
                t = Tile(group, place, RING)
                return None if isinstance(group, int) and not 0 <= t.index < FT else t

            def run(s):
                slot(at(s, 0), at(s, 1), at(s, 2), at(s, 3), at(s, -2))

            ahead = RING + 3
            looped = (FT - 2 - ahead) // RING
            for s in range(ahead):
                run((s // RING, s % RING))
            with eng.Fori(1, 1 + looped) as g:
                for n in range(3, RING + 3):
                    run((g + n // RING, n % RING))
            for s in range(ahead + looped * RING, FT + 3):
                run((s // RING, s % RING))

        block = ctx.enter_context(nc.Block())

        @block.sync
        def _(sp):
            def load(dst, src, done):
                sp.dma_start(dst, src).then_inc(done, 16)

            def load_first(a):
                wait_before(sp, s_ready, a, 2)
                wait_before(sp, s_scaled, a, 2)
                wait_before(sp, r1_ready, a, 2)
                load(xt[a.place][:, :], x_t[:, bass.ts(a.index, P)], x_in[a.place])
                load(xk[a.place][:, :], x_tok[bass.ts(a.index, P), :], x_in[a.place])
                for n in range(2):
                    load(scale_bc[a.place][n * S:(n + 1) * S, :],
                         x_scale[bass.ds(a.index * 2 + n, 1), :].to_broadcast([S, T]), x_in[a.place])

            def load_expert(e):
                for dst, src, width in ((w1_sb, w1, F), (w2_sb, w2, FB * D), (b1_bc, b1.to_broadcast([P, E * F]), F),
                                        (b2_bc, b2.to_broadcast([P, E * D]), D)):
                    load(dst[:, bass.ts(e, width)], src[:, bass.ts(e, width)], weights_in)

            def slot(a, p, q, r, w, c):
                if a:
                    after = Tile(a.group + (a.place + 1) // 2, 1 - a.place)
                    if not isinstance(after.index, int) or after.index < NT:
                        load_first(after)
                    wait_before(sp, v_ready, a, 2)
                    wait_before(sp, sc_masked, a, 2)
                    load(ct[a.place][:, :, :].rearrange("p n k -> p (n k)"), ctx_t[:, bass.ts(a.index, 2 * P)],
                         ctx_in[a.place])
                    load(mk[a.place][:, :], mask[bass.ts(a.index, P), :], ctx_in[a.place])
                    if isinstance(a.index, int) and a.index == 0:
                        for dst, src in ((w_qk[:, 0, :], wq), (w_qk[:, 1, :], wk), (w_qk[:, 2, :], wq_swap),
                                         (w_qk[:, 3, :], wk_swap), (w_v[:, :], wv), (w_o[:, :], wo),
                                         (bo_bc[:, :], bo.to_broadcast([P, D])), (r_w[:, :], router_w),
                                         (r_b[:, :], router_b.to_broadcast([P, E]))):
                            load(dst, src, proj_in)
                    if isinstance(a.index, int) and 2 <= a.index < STAGES:
                        for e in range(2 * (a.index - 2), 2 * (a.index - 1)):
                            load_expert(e)
                if w:
                    sp.wait_ge(x2_ready, w.done)
                    sp.dma_start(x2_dram[bass.ts(w.index, P), :], x2[w.place][:, :]).then_inc(x2_stored[w.place], 16)

            load(kt_sb[:, :], attn_kt, keys_in)
            load_first(Tile(0, 0))
            load(cst[:, :], consts, consts_in)
            load(v_sb[:, :, :], attn_v, consts_in)
            pipeline(sp, slot, NT // 2 - 1)

        CONSTS = 2 * 16
        PROJ = 9 * 16
        WEIGHTS = E * 4 * 16

        @block.tensor
        def _(pe):
            def score_rows(q, groups):
                for g in groups:
                    rows = slice(g * 32, g * 32 + 32)
                    col = (g % 2) * BANK + (g // 2) * GROUP_KEYS
                    for n in range(2):
                        mm = nc.tensor.matmul(ps_sc[n * S:(n + 1) * S, col:col + GROUP_KEYS],
                                              qkt[q.place][rows, n * S:(n + 1) * S],
                                              kbd[q.place][rows, n].rearrange("p h k -> p (h k)"),
                                              start=True, stop=True, tile_position=(g * 32, n * S))
                return mm

            def slot(a, p, q, r, w, c):
                if a and isinstance(a.index, int) and a.index == 0:
                    pe.wait_ge(consts_in, CONSTS)
                if a:
                    pe.wait_ge(x_in[a.place], (a.group + 1) * 64)
                    wait_before(pe, s_scaled, a)
                    nc.tensor.matmul(ps_s[:, :], xt[a.place][:, :], kt_sb[:, :], start=True,
                                     stop=True).then_inc(s_ready, 1)
                if q:
                    pe.wait_ge(kbd_ready, q.index * 2 + 2)
                    wait_before(pe, sc_masked, q)
                    score_rows(q, (0, 1)).then_inc(sc_half, 1)
                if p:
                    pe.wait_ge(x1_ready, p.done)
                    wait_before(pe, rope_ready, p)
                    if c:
                        wait_before(pe, x2t_copied, c)
                    nc.tensor.transpose(ps_x1t, x1[p.place][:, :], ident).then_inc(x1t_ready, 1)
                if c:
                    pe.wait_ge(x2_ready, c.done)
                    if not p:
                        pe.wait_ge(rope_ready, NT)
                        wait_before(pe, x2t_copied, c)
                    nc.tensor.transpose(ps_x2t, x2[c.place][:, :], ident).then_inc(x2t_ready, 1)
                if w:
                    pe.wait_ge(ao_ready, w.done)
                    nc.tensor.transpose(ps_aot, ao[:, :, :].rearrange("p h d -> p (h d)"), ident).then_inc(aot_ready, 1)
                if q:
                    if isinstance(q.index, int) and q.index == 0:
                        pe.wait_ge(proj_in, PROJ)
                    pe.wait_ge(ctx_in[q.place], (q.group + 1) * 32)
                    wait_before(pe, v_copied, q)
                    if c:
                        wait_before(pe, log_copied, c)
                    for n in range(2):
                        mm = nc.tensor.matmul(ps_v[:, n * D:(n + 1) * D], ct[q.place][:, n, :], w_v[:, :],
                                              start=True, stop=True)
                    mm.then_inc(v_ready, 1)
                if c:
                    pe.wait_ge(x2t_copied, c.done)
                    if not q:
                        pe.wait_ge(v_copied, NT)
                        wait_before(pe, log_copied, c)
                    nc.tensor.matmul(ps_log, x2t[:, :], r_w[:, :], start=True, stop=True).then_inc(log_ready, 1)
                if w:
                    pe.wait_ge(aot_copied, w.done)
                    nc.tensor.matmul(ps_wo, aot[:, :], w_o[:, :], start=True, stop=True).then_inc(wo_ready, 1)
                if q:
                    pe.wait_ge(sc_half, q.done)
                    score_rows(q, (2, 3)).then_inc(sc_ready, 1)
                if p:
                    if isinstance(p.index, int) and p.index == 0:
                        pe.wait_ge(proj_in, PROJ)
                    pe.wait_ge(ctx_in[p.place], (p.group + 1) * 32)
                    pe.wait_ge(x1t_copied, p.done)
                    if c:
                        pe.wait_ge(x2t_copied, c.done)
                    for n in range(2):
                        nc.tensor.matmul(ps_p[:, (2 * n + 1) * P:(2 * n + 2) * P], w_qk[:, 2 * n + 1, :],
                                         ct[p.place][:, :, 0:S], start=True, stop=True)
                        mm = nc.tensor.matmul(ps_p[:, 2 * n * P:(2 * n + 1) * P], w_qk[:, 2 * n, :], x1t[:, :],
                                              start=True, stop=True)
                    mm.then_inc(q_ready, 1)
                if a:
                    pe.wait_ge(p_ready, a.done)
                    wait_before(pe, r1_ready, a)
                    for t in range(TB):
                        mm = nc.tensor.transpose(ps_pt[:, t * P:(t + 1) * P], p_sb[:, t * P:(t + 1) * P], ident)
                    mm.then_inc(pt_ready, 1)
                if r:
                    pe.wait_ge(pb_ready, r.done)
                    if w:
                        pe.wait_ge(r2_ready, w.done)
                    for h in range(HPAIR):
                        mm = nc.tensor.transpose(ps_bt[:, h * P:(h + 1) * P], pb_sb[r.place][:, h * P:(h + 1) * P],
                                                 ident)
                        if h % (HPAIR // 2) == HPAIR // 2 - 1:
                            mm.then_inc(bt_ready, 1)
                if a:
                    pe.wait_ge(pt_copied, a.done)
                    for t in range(TB):
                        mm = nc.tensor.matmul(ps_o, pt_sb[:, t * P:(t + 1) * P], v_sb[:, t, :], start=(t == 0),
                                              stop=(t == TB - 1))
                    mm.then_inc(o_ready, 1)
                if r:
                    for h in range(HPAIR):
                        if h % (HPAIR // 2) == 0:
                            pe.wait_ge(bt_copied, r.index * 2 + (1 + h // (HPAIR // 2)))
                        mm = nc.tensor.matmul(ps_bo[:, h * 2 * VA:(h + 1) * 2 * VA], pbt[:, h * P:(h + 1) * P],
                                              vaug[r.place][:, h].rearrange("p n c -> p (n c)"), start=True, stop=True)
                    mm.then_inc(bo_ready, 1)

            def expert_slot(x, h, y, done, ahead):
                if x:
                    pe.wait_ge(xs_in[x.place], x.landed)
                    wait_before(pe, xst_copied, x)
                    nc.tensor.transpose(ps_xs, xs[x.place][:, :], ident).then_inc(xst_ready, 1)
                if y:
                    pe.wait_ge(h_added, y.done)
                    wait_before(pe, ht_copied, y, 2)
                    for f in range(FB):
                        mm = nc.tensor.transpose(ps_ht[y.place % 2][:, f * P:(f + 1) * P],
                                                 h_sb[y.place % 2][:, f * P:(f + 1) * P], ident)
                    mm.then_inc(ht_ready, 1)
                if h:
                    expert = pe.value_load(expert_of[0:1, bass.ds(h.index, 1)], min_val=0, max_val=E - 1)
                    pe.wait_ge(xst_copied, h.done)
                    wait_before(pe, h_added, h, 2)
                    nc.tensor.matmul(ps_h[h.place % 2], xst[h.place % 2][:, :], w1_sb[:, bass.ts(expert, F)],
                                     start=True, stop=True).then_inc(h_ready, 1)
                if y:
                    expert = pe.value_load(expert_of[0:1, bass.ds(y.index, 1)], min_val=0, max_val=E - 1)
                    pe.wait_ge(ht_copied, y.done)
                    wait_before(pe, yb_ready, y, 2)
                    for f in range(FB):
                        mm = nc.tensor.matmul(ps_y[y.place % 2], ht_sb[y.place % 2][:, f * P:(f + 1) * P],
                                              w2_sb[:, bass.ds(expert * (FB * D) + f * D, D)], start=(f == 0),
                                              stop=(f == FB - 1))
                    mm.then_inc(y_ready, 1)

            pe.wait_ge(keys_in, 16)
            pipeline(pe, slot)

            pe.wait_ge(chosen_ready, 1)
            pe.wait_ge(pool_ones, 1)
            pe.wait_ge(setup_done, 2)
            hot = chosen_bf[:, :, :].rearrange("p t e -> p (t e)")
            nc.tensor.matmul(ps_rank, tri_bf[:, :], hot, start=True, stop=False)
            for t in range(1, NT):
                nc.tensor.matmul(ps_rank[:, t * E:], ones_bf[:, :], hot[:, 0:(NT - t) * E], start=False,
                                 stop=(t == NT - 1))
            for t in range(NT):
                mm = nc.tensor.matmul(ps_count, ones_bf[:, :], hot[:, t * E:(t + 1) * E], start=(t == 0),
                                      stop=(t == NT - 1))
            mm.then_inc(rank_ready, 1)
            pe.wait_ge(hot_ready, 1)
            for t in range(NT):
                mm = nc.tensor.matmul(ps_sorted, lane_hot[:, t, :],
                                      tile_vals[:, t].rearrange("p v j -> p (v j)"), start=(t == 0), stop=(t == NT - 1))
            mm.then_inc(sorted_ready, 1)
            pe.wait_ge(routed, 1)
            pe.wait_ge(weights_in, WEIGHTS)
            expert_pipeline(pe, expert_slot)

        @block.scalar
        def _(act):
            def slot(a, p, q, r, w, c):
                if p:
                    act.wait_ge(x1t_ready, p.done)
                    if c:
                        act.wait_ge(x2t_ready, c.done)
                    wait_before(act, q_ready, p)
                    nc.scalar.copy(x1t[:, :], ps_x1t).then_inc(x1t_copied, 1)
                if c:
                    act.wait_ge(x2t_ready, c.done)
                    wait_before(act, log_ready, c)
                    nc.scalar.copy(x2t[:, :], ps_x2t).then_inc(x2t_copied, 1)
                if w:
                    act.wait_ge(aot_ready, w.done)
                    wait_before(act, wo_ready, w)
                    nc.scalar.copy(aot[:, :], ps_aot).then_inc(aot_copied, 1)
                if a:
                    act.wait_ge(nmax_ready, a.done)
                    wait_before(act, pt_ready, a)
                    wait_before(act, pinv_ready, a)
                    nc.scalar.activation(p_sb[:, :], s_sb[:, :], ACT.Exp, bias=s_nmax[:, :],
                                         accum_out=p_sum[:, :]).then_inc(p_ready, 1)
                if r:
                    act.wait_ge(sd_ready, r.done)
                    nc.scalar.activation(pb_sb[r.place][:, :], sd_sb[:, :, :].rearrange("p h k -> p (h k)"),
                                         ACT.Exp).then_inc(pb_ready, 1)
                if a:
                    act.wait_ge(pt_ready, a.done)
                    wait_before(act, o_ready, a)
                    nc.scalar.copy(pt_sb[:, :], ps_pt[:, :]).then_inc(pt_copied, 1)
                if r:
                    for n in range(2):
                        act.wait_ge(bt_ready, r.index * 2 + (1 + n))
                        if n == 0:
                            wait_before(act, bo_ready, r)
                        nc.scalar.copy(pbt[:, n * BANK:(n + 1) * BANK],
                                       ps_bt[:, n * BANK:(n + 1) * BANK]).then_inc(bt_copied, 1)
                if p:
                    act.wait_ge(qk_ready, p.done)
                    wait_before(act, sc_ready, p, 2)
                    for h in range(HG):
                        mm = nc.scalar.activation(kbd[p.place][:, :, h, :],
                                                  qkt[p.place][:, P:2 * P].rearrange("p (n k) -> p n k", n=2),
                                                  ACT.Copy, scale=cst[:, C_HM + h:C_HM + h + 1])
                        if h % 2 == 1:
                            mm.then_inc(kbd_ready, 1)

            def name_rows(j):
                nc.scalar.copy(from_cur[j.place][:, :], from_row[:, bass.ds(j.index, 1)]).then_inc(from_copied, 1)

            def expert_slot(x, h, y, done, ahead):
                if ahead and not (isinstance(ahead.index, int) and ahead.index < RING):
                    act.wait_ge(xs_in[ahead.place], ahead.group * 16)
                    name_rows(ahead)
                if x:
                    act.wait_ge(xst_ready, x.done)
                    wait_before(act, h_ready, x, 2)
                    nc.scalar.copy(xst[x.place % 2][:, :], ps_xs).then_inc(xst_copied, 1)
                if y:
                    act.wait_ge(ht_ready, y.done)
                    wait_before(act, y_ready, y, 2)
                    nc.scalar.activation(ht_sb[y.place % 2][:, :], ps_ht[y.place % 2],
                                         ACT.Relu).then_inc(ht_copied, 1)
                if done:
                    if not (isinstance(done.group, int) and done.group == 0):
                        act.wait_ge(out_stored[done.place], done.group * 16)
                    nc.scalar.copy(to_cur[done.place][:, :], to_row[:, bass.ds(done.index, 1)]
                                   ).then_inc(to_copied, 1)

            act.wait_ge(consts_in, CONSTS)
            pipeline(act, slot)
            act.wait_ge(shifted, 1)
            nc.scalar.activation(lg_exp[:, :, :].rearrange("p t e -> p (t e)"),
                                 lg_sub[:, :, :].rearrange("p t e -> p (t e)"), ACT.Exp).then_inc(exp_ready, 1)
            act.wait_ge(routed, 1)
            for n in range(RING):
                name_rows(Tile(0, n, RING))
            expert_pipeline(act, expert_slot)

        @block.vector
        def _(dve):
            def moments(r, stats, mv, stats_done, var_ready, tile):
                nc.vector.bn_stats(stats[:, :], r[:, :]).then_inc(stats_done, 1)
                dve.wait_ge(stats_done, tile.done)
                carry(dve, dve_passed)
                nc.vector.bn_aggr(mv[:, :], stats[:, :]).then_inc(var_ready, 1)

            def slot(a, p, q, r, w, c):
                if a:
                    dve.wait_ge(s_ready, a.done)
                    dve.wait_ge(x_in[a.place], (a.group + 1) * 64)
                    wait_before(dve, p_ready, a)
                    carry(dve, dve_passed)
                    nc.vector.tensor_tensor_reduce(out=s_sb[:, :], in0=ps_s[:, :], in1=scale_bc[a.place][:, :],
                                                   scale=1.0, scalar=-3.0e38, op0=ALU.mult, op1=ALU.max,
                                                   accum_out=s_max[:, :]).then_inc(s_scaled, 1)
                    dve.wait_ge(s_scaled, a.done)
                    nc.vector.tensor_scalar(s_nmax[:, :], s_max[:, :], -1.0, None, ALU.mult).then_inc(nmax_ready, 1)
                if q:
                    dve.wait_ge(v_ready, q.done)
                    if c:
                        dve.wait_ge(log_ready, c.done)
                    wait_before(dve, bo_ready, q, 2)
                    for n in range(2):
                        rows = slice(n * S, (n + 1) * S)
                        for m in range(2):
                            src = ps_v[rows, m * D:(m + 1) * D].rearrange("p (g h d) -> p g h d", h=2, d=HD)
                            cp = nc.vector.tensor_copy(
                                vaug[q.place][rows, :, m, n * (HD + 1):n * (HD + 1) + HD], src[:, :, n, :])
                    cp.then_inc(v_copied, 1)
                if c:
                    dve.wait_ge(log_ready, c.done)
                    nc.vector.tensor_tensor(logits[:, bass.ds(c.index, 1), :].rearrange("p t e -> p (t e)"), ps_log,
                                            r_b[:, :], ALU.add).then_inc(log_copied, 1)
                if w:
                    dve.wait_ge(wo_ready, w.done)
                    nc.vector.tensor_tensor(r2[:, :], ps_wo, x1b[:, bass.ts(w.index, D)], ALU.add).then_inc(r2_ready, 1)
                    dve.wait_ge(r2_ready, w.done)
                    moments(r2, st2, mv2, st2_ready, var2_ready, w)
                if q:
                    dve.wait_ge(sc_ready, q.done)
                    dve.wait_ge(sc_filled, q.done)
                    dve.wait_ge(ctx_in[q.place], (q.group + 1) * 32)
                    carry(dve, dve_passed)
                    for n in range(2):
                        keep = mk[q.place][:, :].unsqueeze(1).unsqueeze(1).to_broadcast([P, 2, HG, S])
                        into = sc_sb[:, :, :].rearrange("p (m n h) k -> p n m h k", m=2, n=2)[:, n]
                        cp = nc.vector.copy_predicated(
                            into, keep, ps_sc[:, n * BANK:(n + 1) * BANK].rearrange("p (m h k) -> p m h k", m=2, k=S))
                    cp.then_inc(sc_masked, 1)
                if p:
                    dve.wait_ge(q_ready, p.done)
                    wait_before(dve, qk_ready, p)
                    nc.vector.tensor_tensor(rope_c[:, :], ps_p[:, 0:2 * P], cst[:, C_COS:C_COS + 2 * P], ALU.mult)
                    nc.vector.tensor_tensor(rope_s[:, :], ps_p[:, 2 * P:4 * P], cst[:, C_SIN:C_SIN + 2 * P],
                                            ALU.mult).then_inc(rope_ready, 1)
                if w:
                    if not (isinstance(w.group, int) and w.group == 0):
                        dve.wait_ge(x2_stored[w.place], w.group * 16)
                    wait_before(dve, x2t_ready, w, 2)
                    dve.wait_ge(rstd2_ready, w.done)
                    nc.vector.tensor_scalar(x2[w.place][:, :], r2[:, :], mv2[:, 0:1], rstd2[:, 0:1], ALU.subtract,
                                            ALU.mult).then_inc(x2_ready, 1)
                if q:
                    dve.wait_ge(sc_masked, q.done)
                    wait_before(dve, sd_ready, q)
                    nc.vector.tensor_reduce(sc_max[:, :], sc_sb[:, :, :], AX.X, ALU.max).then_inc(scmax_ready, 1)
                if a:
                    dve.wait_ge(p_ready, a.done)
                    nc.vector.reciprocal(p_inv[:, :], p_sum[:, :]).then_inc(pinv_ready, 1)
                    dve.wait_ge(pinv_ready, a.done)
                    dve.wait_ge(o_ready, a.done)
                    nc.vector.scalar_tensor_tensor(out=r1[:, :], in0=ps_o, scalar=p_inv[:, 0:1],
                                                   in1=xk[a.place][:, :], op0=ALU.mult, op1=ALU.add).then_inc(r1_ready, 1)
                    dve.wait_ge(r1_ready, a.done)
                    moments(r1, st1, mv1, st1_ready, var1_ready, a)
                if r:
                    dve.wait_ge(bo_ready, r.done)
                    wait_before(dve, aot_ready, r)
                    views = [ps_bo[n * S:(n + 1) * S, :].rearrange("p (g n h c) -> p g n h c", n=2, h=2, c=HD + 1)
                             [:, :, n] for n in range(2)]
                    for n in range(2):
                        rc = nc.vector.reciprocal(
                            ao_inv[n * S:(n + 1) * S, :].rearrange("p (g h) -> p g h", h=2), views[n][:, :, :, HD])
                    rc.then_inc(ao_inv_ready, 1)
                    dve.wait_ge(ao_inv_ready, r.done)
                    for n in range(2):
                        rows = slice(n * S, (n + 1) * S)
                        inv = ao_inv[rows, :].rearrange("p (g h) -> p g h", h=2)
                        ml = nc.vector.tensor_tensor(ao[rows].rearrange("p (g h) d -> p g h d", h=2),
                                                     views[n][:, :, :, 0:HD], spread(inv, 3, [S, HPAIR, 2, HD]), ALU.mult)
                    ml.then_inc(ao_ready, 1)
                if a:
                    wait_before(dve, x1t_ready, a, 2)
                    wait_before(dve, x1b_ready, a, 2)
                    dve.wait_ge(rstd1_ready, a.done)
                    nc.vector.tensor_scalar(x1[a.place][:, :], r1[:, :], mv1[:, 0:1], rstd1[:, 0:1], ALU.subtract,
                                            ALU.mult).then_inc(x1_ready, 1)

            def routing():
                steps = [0]

                def then(ins):
                    steps[0] += 1
                    ins.then_inc(route, 1)
                    dve.wait_ge(route, steps[0])

                v = nc.vector
                dve.wait_ge(log_copied, NT)
                then(v.tensor_reduce(lg_max[:, :], logits[:, :, :], AX.X, ALU.max))
                v.tensor_tensor(lg_sub[:, :, :], logits[:, :, :], spread(lg_max[:, :], 2, [P, NT, E]),
                                ALU.subtract).then_inc(shifted, 1)
                then(v.tensor_tensor(at_max[:, :, :], logits[:, :, :], spread(lg_max[:, :], 2, [P, NT, E]),
                                     ALU.is_ge))
                weight8 = spread(cst[:, C_W8:C_W8 + E], 1, [P, NT, E])
                then(v.tensor_tensor(chosen[:, :, :], at_max[:, :, :], weight8, ALU.mult))
                then(v.tensor_reduce(first[:, :], chosen[:, :, :], AX.X, ALU.max))
                then(v.tensor_tensor(chosen[:, :, :], weight8, spread(first[:, :], 2, [P, NT, E]), ALU.is_equal))
                v.tensor_copy(chosen_bf[:, :, :], chosen[:, :, :]).then_inc(chosen_ready, 1)
                dve.wait_ge(exp_ready, 1)
                then(v.tensor_reduce(first[:, :], lg_exp[:, :, :], AX.X, ALU.add))
                then(v.reciprocal(gate[:, :], first[:, :]))
                then(v.tensor_copy(vals[:, :, 0:2],
                                   cst[:, C_TOK:C_TOK + 2 * NT].rearrange("p (t v) -> p t v", v=2)))
                then(v.tensor_copy(vals[:, :, 2], gate[:, :]))
                then(v.tensor_tensor(gate_rest[:, :], gate[:, :], vals[:, :, 2], ALU.subtract))
                then(v.tensor_copy(vals[:, :, 3], gate_rest[:, :]))
                then(v.tensor_tensor(gate[:, :], gate_rest[:, :], vals[:, :, 3], ALU.subtract))
                then(v.tensor_copy(vals[:, :, 4], gate[:, :]))
                dve.wait_ge(rank_ready, 1)
                then(v.tensor_scalar(whole[:, :], ps_count, float(P - 1), None, ALU.add))
                then(v.tensor_copy(whole_i[:, :], whole[:, :]))
                then(v.tensor_scalar(whole_i[:, :], whole_i[:, :], 7, None, ALU.arith_shift_right))
                then(v.tensor_copy(whole[:, :], whole_i[:, :]))
                then(v.tensor_copy(ends[:, 0:1], whole[:, 0:1]))
                for e in range(1, E):
                    then(v.tensor_tensor(ends[:, e:e + 1], ends[:, e - 1:e], whole[:, e:e + 1], ALU.add))
                then(v.tensor_tensor(starts[:, :], ends[:, :], whole[:, :], ALU.subtract))
                then(v.tensor_scalar(starts[:, :], starts[:, :], float(P), None, ALU.mult))
                then(v.tensor_tensor(place_e[:, :, :], ps_rank.rearrange("p (t e) -> p t e", e=E),
                                     spread(starts[:, :], 1, [P, NT, E]), ALU.add))
                then(v.tensor_tensor(place_e[:, :, :], place_e[:, :, :], chosen[:, :, :], ALU.mult))
                then(v.tensor_reduce(place_f[:, :], place_e[:, :, :], AX.X, ALU.add))
                then(v.tensor_copy(place_i[:, :], place_f[:, :]))
                then(v.tensor_scalar(part_i[:, :], place_i[:, :], P - 1, None, ALU.bitwise_and))
                then(v.tensor_copy(lane_f[:, :], part_i[:, :]))
                then(v.tensor_scalar(part_i[:, :], place_i[:, :], 7, None, ALU.arith_shift_right))
                then(v.tensor_copy(tile_f[:, :], part_i[:, :]))
                then(v.tensor_tensor(tile_hot[:, :, :], spread(cst[:, C_IOTA:C_IOTA + FT], 1, [P, NT, FT]),
                                     spread(tile_f[:, :], 2, [P, NT, FT]), ALU.is_equal))
                then(v.tensor_tensor(tile_vals[:, :, :, :], spread(tile_hot[:, :, :], 2, [P, NT, VALS, FT]),
                                     spread(vals[:, :, :], 3, [P, NT, VALS, FT]), ALU.mult))
                v.tensor_tensor(lane_hot[:, :, :], spread(cst[:, C_IOTA:C_IOTA + P], 1, [P, NT, P]),
                                spread(lane_f[:, :], 2, [P, NT, P]), ALU.is_equal).then_inc(hot_ready, 1)
                then(v.tensor_tensor(past[:, :, :], spread(cst[:, C_IOTA:C_IOTA + FT], 2, [P, FT, E]),
                                     spread(ends[:, :], 1, [P, FT, E]), ALU.is_ge))
                then(v.tensor_reduce(expert_f[:, :], past[:, :, :], AX.X, ALU.add))
                then(v.tensor_scalar(expert_low[:, :], expert_f[:, :], float(E - 1), None, ALU.min))
                then(v.tensor_copy(expert_of[:, :], expert_low[:, :]))
                dve.wait_ge(sorted_ready, 1)
                then(v.tensor_copy(sorted_sb[:, :, :].rearrange("p v j -> p (v j)"), ps_sorted))
                then(v.scalar_tensor_tensor(out=row_f[:, :], in0=sorted_sb[:, 0, :], scalar=float(P),
                                            in1=sorted_sb[:, 1, :], op0=ALU.mult, op1=ALU.add))
                then(v.tensor_scalar(from_f[:, :], row_f[:, :], -float(P), 0.0, ALU.add, ALU.max))
                then(v.tensor_copy(from_row[:, :], from_f[:, :]))
                then(v.tensor_scalar(to_f[:, :], sorted_sb[:, 0, :], 0.5, float(2 * NT * P), ALU.is_lt, ALU.mult))
                then(v.tensor_tensor(to_f[:, :], to_f[:, :], from_f[:, :], ALU.add))
                then(v.tensor_copy(to_row[:, :], to_f[:, :]))
                then(v.tensor_tensor(gate_sum[:, :], sorted_sb[:, 3, :], sorted_sb[:, 4, :], ALU.add))
                v.tensor_tensor(sorted_gate[:, :], sorted_sb[:, 2, :], gate_sum[:, :], ALU.add).then_inc(routed, 1)
                dve.wait_ge(routed, 1)

            def expert_slot(x, h, y, done, ahead):
                if h:
                    expert = dve.value_load(expert_of[0:1, bass.ds(h.index, 1)], min_val=0, max_val=E - 1)
                    dve.wait_ge(h_ready, h.done)
                    wait_before(dve, ht_ready, h, 2)
                    nc.vector.tensor_tensor(h_sb[h.place % 2][:, :], ps_h[h.place % 2],
                                            b1_bc[:, bass.ts(expert, F)], ALU.add).then_inc(h_added, 1)
                if y:
                    expert = dve.value_load(expert_of[0:1, bass.ds(y.index, 1)], min_val=0, max_val=E - 1)
                    dve.wait_ge(y_ready, y.done)
                    wait_before(dve, r3_ready, y)
                    nc.vector.tensor_tensor(yb[:, :], ps_y[y.place % 2], b2_bc[:, bass.ts(expert, D)],
                                            ALU.add).then_inc(yb_ready, 1)
                if done:
                    dve.wait_ge(rstd3_ready, done.done)
                    if not (isinstance(done.group, int) and done.group == 0):
                        dve.wait_ge(out_stored[done.place], done.group * 16)
                    nc.vector.tensor_scalar(res[done.place][:, :], r3[done.place % 2][:, :],
                                            mv3[done.place % 2][:, 0:1], rstd3[done.place % 2][:, 0:1], ALU.subtract,
                                            ALU.mult).then_inc(res_ready, 1)
                if y:
                    dve.wait_ge(yb_ready, y.done)
                    wait_before(dve, res_ready, y, 2)
                    nc.vector.scalar_tensor_tensor(out=r3[y.place % 2][:, :], in0=yb[:, :],
                                                   scalar=sorted_gate[:, bass.ds(y.index, 1)], in1=xs[y.place][:, :],
                                                   op0=ALU.mult, op1=ALU.add).then_inc(r3_ready, 1)
                    dve.wait_ge(r3_ready, y.done)
                    nc.vector.bn_stats(st3[:, :], r3[y.place % 2][:, :]).then_inc(st3_ready, 1)
                    dve.wait_ge(st3_ready, y.done)
                    carry(dve, dve_passed)
                    nc.vector.bn_aggr(mv3[y.place % 2][:, :], st3[:, :]).then_inc(var3_ready, 1)

            dve.wait_ge(consts_in, CONSTS)
            for n in range(2):
                cp = nc.vector.tensor_copy(vaug[n][:, :, :, :].rearrange("p g n c -> p (g n c)"),
                                           cst[:, C_VA:C_VA + 2 * HPAIR * VA])
            cp.then_inc(setup_done, 1)
            nc.vector.tensor_copy(tri_bf[:, :], cst[:, C_TRI:C_TRI + P]).then_inc(setup_done, 1)
            dve.wait_ge(setup_done, 2)
            dve.wait_ge(proj_in, PROJ)
            pipeline(dve, slot)
            routing()
            dve.wait_ge(weights_in, WEIGHTS)
            expert_pipeline(dve, expert_slot)

        @block.gpsimd
        def _(pool):
            def root(var, ve, ready_var, ve_ready, rstd, rstd_ready, tile):
                pool.wait_ge(ready_var, tile.done)
                carry(pool, pool_passed)
                nc.gpsimd.tensor_scalar(ve[:, :], var, EPS, 1.0, ALU.add, ALU.mult).then_inc(ve_ready, 1)
                pool.wait_ge(ve_ready, tile.done)
                nc.gpsimd.tensor_tensor(rstd[:, :], ve[:, :], half_neg[:, :], ALU.pow).then_inc(rstd_ready, 1)

            def slot(a, p, q, r, w, c):
                if q:
                    wait_before(pool, sd_ready, q)
                    carry(pool, pool_passed)
                    nc.gpsimd.memset(sc_sb[:, :, :], MASKED).then_inc(sc_filled, 1)
                if p:
                    pool.wait_ge(x1_ready, p.done)
                    nc.gpsimd.tensor_tensor(x1b[:, bass.ts(p.index, D)], x1[p.place][:, :], bo_bc[:, :],
                                            ALU.add).then_inc(x1b_ready, 1)
                if w:
                    root(mv2[:, 1:2], ve2, var2_ready, ve2_ready, rstd2, rstd2_ready, w)
                if p:
                    pool.wait_ge(rope_ready, p.done)
                    wait_before(pool, sc_ready, p, 2)
                    nc.gpsimd.tensor_tensor(qkt[p.place][:, :], rope_c[:, :], rope_s[:, :], ALU.add).then_inc(qk_ready, 1)
                if a:
                    root(mv1[:, 1:2], ve1, var1_ready, ve1_ready, rstd1, rstd1_ready, a)
                if q:
                    pool.wait_ge(scmax_ready, q.done)
                    wait_before(pool, pb_ready, q)
                    nc.gpsimd.tensor_tensor(sd_sb[:, :, :], sc_sb[:, :, :], spread(sc_max[:, :], 2, [P, HEADS, S]),
                                            ALU.subtract).then_inc(sd_ready, 1)

            def gather(j):
                wait_before(pool, r3_ready, j, RING)
                pool.wait_ge(from_copied, j.done)
                carry(pool, pool_passed)
                pool.indirect_dma_start(xs[j.place][:, :], None, x2_dram,
                                        bass.IndirectOffsetOnAxis(from_cur[j.place][:, :], 0)
                                        ).then_inc(xs_in[j.place], 16)

            def expert_slot(x, h, y, done, ahead):
                if ahead and not (isinstance(ahead.index, int) and ahead.index < RING):
                    gather(ahead)
                if y:
                    root(mv3[y.place % 2][:, 1:2], ve3, var3_ready, ve3_ready, rstd3[y.place % 2], rstd3_ready, y)
                if done:
                    pool.wait_ge(to_copied, done.done)
                    pool.wait_ge(res_ready, done.done)
                    carry(pool, pool_passed)
                    pool.indirect_dma_start(out, bass.IndirectOffsetOnAxis(to_cur[done.place][:, :], 0),
                                            res[done.place][:, :], None, bounds_check=NT * P - 1, oob_is_err=False
                                            ).then_inc(out_stored[done.place], 16)

            nc.gpsimd.memset(ones_bf[:, :], 1.0).then_inc(pool_ones, 1)
            nc.gpsimd.memset(half_neg[:, :], -0.5).then_inc(pool_setup, 1)
            pool.wait_ge(pool_setup, 1)
            pool.wait_ge(proj_in, PROJ)
            pipeline(pool, slot)
            pool.wait_ge(routed, 1)
            for n in range(2):
                pool.wait_ge(x2_stored[n], NT // 2 * 16)
            for n in range(RING):
                gather(Tile(0, n, RING))
            expert_pipeline(pool, expert_slot)
            for n in range(RING):
                pool.wait_ge(out_stored[n], len(range(n, FT, RING)) * 16)


_IN = ["x_tok", "x_t", "x_scale", "ctx_t", "mask", "attn_kt", "attn_v", "wq", "wq_swap", "wk", "wk_swap", "wv", "wo",
       "bo", "router_w", "router_b", "w1", "b1", "w2", "b2", "consts"]


def _constants():
    import numpy as np

    c = np.zeros((P, C_ALL), np.float32)
    c[:, C_ID:C_ID + P] = np.eye(P)
    inv_freq = (1.0 / np.float32(10000.0) ** (np.arange(0, HD, 2, dtype=np.float32) / np.float32(HD))).astype(np.float32)
    angle = (np.arange(S, dtype=np.float32)[:, None] * inv_freq[None, :]).astype(np.float32)
    feature = np.arange(P)
    pair = (feature % HD) // 2
    cos, sin = np.cos(angle)[:, pair].T, np.sin(angle)[:, pair].T
    sin = sin * np.where(feature % 2 == 0, -1.0, 1.0)[:, None]
    root = np.float32(1.0 / np.sqrt(HD))
    for n in range(2):
        c[:, C_COS + n * S:C_COS + (n + 1) * S] = cos * root
        c[:, C_COS + P + n * S:C_COS + P + (n + 1) * S] = cos
        c[:, C_SIN + n * S:C_SIN + (n + 1) * S] = sin * root
        c[:, C_SIN + P + n * S:C_SIN + P + (n + 1) * S] = sin
    c[feature, C_HM + (feature // HD) % HG] = 1.0
    va = np.zeros((P, HPAIR * 2, VA), np.float32)
    va[:S, :, HD] = 1.0
    va[S:, :, 2 * HD + 1] = 1.0
    c[:, C_VA:C_VA + 2 * HPAIR * VA] = va.reshape(P, -1)
    c[:, C_TRI:C_TRI + P] = feature[:, None] < feature[None, :]
    c[:, C_IOTA:C_IOTA + P] = feature[None, :]
    c[:, C_W8:C_W8 + E] = E - np.arange(E)[None, :]
    tok = np.zeros((P, NT, 2), np.float32)
    tok[:, :, 0] = np.arange(NT)[None, :] + 1
    tok[:, :, 1] = feature[:, None]
    c[:, C_TOK:C_TOK + 2 * NT] = tok.reshape(P, -1)
    return c


def kernel(**inputs):
    import numpy as np
    import concourse.bacc as bacc
    from concourse.bass_utils import run_bass_kernel_spmd

    i = {k: np.asarray(v) for k, v in inputs.items()}
    x = i["x"].reshape(NT * P, D)
    swap = np.arange(D) ^ 1
    arrays = {
        "x_tok": x,
        "x_t": x.T,
        "x_scale": i["x"][:, ::S // 4, :].reshape(B, T),
        "ctx_t": np.repeat(i["ctx_1024"][:, None], 2, axis=1).reshape(2 * NT * P, D).T,
        "mask": i["mask_Bx1xSxS2_ik1"].reshape(NT * P, S),
        "attn_kt": i["L0_attn_k"][0].T,
        "attn_v": i["L0_attn_v"][0].reshape(TB, P, D).transpose(1, 0, 2),
        "wq": i["L0_xattn_Wq"], "wq_swap": i["L0_xattn_Wq"][:, swap],
        "wk": i["L0_xattn_Wk"], "wk_swap": i["L0_xattn_Wk"][:, swap],
        "wv": i["L0_xattn_Wv"], "wo": i["L0_xattn_Wo"], "bo": i["L0_xattn_bo"].reshape(1, D),
        "router_w": i["L0_ffn_router_W"], "router_b": i["L0_ffn_router_b"].reshape(1, E),
        "w1": i["L0_ffn_W1"].transpose(1, 0, 2).reshape(P, E * F),
        "b1": i["L0_ffn_b1"].reshape(1, E * F),
        "w2": i["L0_ffn_W2"].reshape(E, FB, P, D).transpose(2, 0, 1, 3).reshape(P, E * FB * D),
        "b2": i["L0_ffn_b2"].reshape(1, E * D),
        "consts": _constants(),
    }
    nc = bacc.Bacc("TRN2", target_bir_lowering=False, num_devices=1)
    feeds, args = {}, []
    for name in _IN:
        a = np.ascontiguousarray(arrays[name])
        feeds[f"in_{name}"] = a
        args.append(nc.dram_tensor(f"in_{name}", a.shape, mybir.dt.from_np(a.dtype), kind="ExternalInput").ap())
    result = nc.dram_tensor("out", (NT * P, D), F32, kind="ExternalOutput").ap()
    decoder_kernel(nc, *args, result)
    r = run_bass_kernel_spmd(nc, [feeds], core_ids=[0])
    return np.asarray(r.results[0]["out"]).reshape(B, S, D)
```

```python
from contextlib import ExitStack

import concourse.bass as bass
from concourse import mybir

ALU = mybir.AluOpType
ACT = mybir.ActivationFunctionType
AX = mybir.AxisListType
F32 = mybir.dt.float32
BF16 = mybir.dt.bfloat16
I32 = mybir.dt.int32
U32 = mybir.dt.uint32

P = 128
B, S, D = 32, 64, 128
NT = B * S // P
NT_EARLY = NT - 2
T = 512
TB = T // P
HEADS, HD = 16, 8
HPAIR = HEADS // 2
RG = 4
HG = HEADS // RG
GROUP_KEYS = HG * S
BANK = 512
CG = 4
OCT = HPAIR // CG
PD = 2 * HD
E, F = 8, 512
FB = F // P
FT = NT + E - 1
NEAR = F + FB + D
RING = 4
POOL_VALS = 10
VALS = 5
EPS = 1e-5
MASKED = -10000.0

C_ID = 0
C_COS = C_ID + P
C_SIN = C_COS + 2 * P
C_HM = C_SIN + 2 * P
C_OWN = C_HM + HG
C_TRI = C_OWN + 4 * PD
C_IOTA = C_TRI + P
C_W8 = C_IOTA + P
C_TOK = C_W8 + E
C_LT = C_TOK + 2 * NT
C_LE = C_LT + E * E
C_ALL = C_LE + E * E


class Tile:

    def __init__(self, group, place, per=2):
        self.group, self.place, self.per = group, place, per

    @property
    def index(self):
        return self.group * self.per + self.place

    @property
    def done(self):
        return self.index + 1

    @property
    def landed(self):
        return (self.group + 1) * 16


def wait_before(eng, sem, tile, back=1):
    if isinstance(tile.index, int) and tile.index < back:
        return
    eng.wait_ge(sem, tile.index + (1 - back))


def carry(eng, passed):
    eng.sem_inc(passed, 1)


def spread(ap, axis, shape):
    return ap.unsqueeze(axis).to_broadcast(shape)


def decoder_kernel(nc, x_tok, x_t, x_scale, ctx_t, mask, attn_kt, attn_v, wq, wq_swap, wk, wk_swap, wv, wo, bo,
                   router_w, router_b, w1, b1, w2, b2, consts, out):
    with ExitStack() as ctx:
        def sb(name, shape, dt=F32):
            return ctx.enter_context(nc.sbuf_tensor(name, shape, dt))

        def psum(name, shape, dt=F32):
            return ctx.enter_context(nc.psum_tensor(name, shape, dt))

        def sem(name):
            return ctx.enter_context(nc.semaphore(name))

        x2_dram = nc.dram_tensor("x2_rows", [NT * P, D], F32, kind="Internal").ap()

        cst = sb("cst", [P, C_ALL])
        ident = cst[:, C_ID:C_ID + P]
        own_keys = cst[:, C_OWN:C_OWN + 4 * PD].rearrange("p (n m c) -> p n m c", n=2, m=2)
        idle_sb = sb("idle_sb", [P, BANK])
        kt_sb = sb("kt_sb", [P, T])
        v_sb = sb("v_sb", [P, TB, D])
        w_qk = sb("w_qk", [P, 4, D])
        w_v = sb("w_v", [P, 2, D // 2])
        w_o = sb("w_o", [P, 2, OCT, D])
        bo_bc = sb("bo_bc", [P, D])
        r_w = sb("r_w", [P, E])
        r_b = sb("r_b", [P, E])

        xt = [sb(f"xt{n}", [P, P]) for n in range(2)]
        xk = [sb(f"xk{n}", [P, D]) for n in range(2)]
        scale_bc = [sb(f"scale_bc{n}", [P, T]) for n in range(2)]
        s_sb = sb("s_sb", [P, T])
        s_max = sb("s_max", [P, 1])
        s_nmax = sb("s_nmax", [P, 1])
        p_sb = sb("p_sb", [P, T])
        p_sum = sb("p_sum", [P, 1])
        p_inv = sb("p_inv", [P, 1])
        pt_sb = sb("pt_sb", [P, T])
        r1 = sb("r1", [P, D])
        st1 = sb("st1", [P, 6])
        mv1 = sb("mv1", [P, 2])
        rstd1 = sb("rstd1", [P, 1])
        x1 = [sb(f"x1_{n}", [P, D]) for n in range(2)]

        ct = [sb(f"ct{n}", [P, P]) for n in range(2)]
        mk = [sb(f"mk{n}", [P, S], I32) for n in range(2)]
        x1b = sb("x1b", [P, NT * D])
        x1t = sb("x1t", [P, P])
        rope_c = sb("rope_c", [P, 2 * P])
        rope_s = sb("rope_s", [P, 2 * P])
        qkt = [sb(f"qkt{n}", [P, 2 * P]) for n in range(2)]
        kbd = [sb(f"kbd{n}", [P, 2, HG, S]) for n in range(2)]
        vz = [sb(f"vz{n}", [P, HPAIR, 2, PD]) for n in range(2)]
        sc_sb = sb("sc_sb", [P, HEADS, S])
        sc_max = sb("sc_max", [P, HEADS])
        sd_sb = sb("sd_sb", [P, HEADS, S])
        pb_sb = [sb(f"pb_sb{n}", [P, HEADS * S]) for n in range(2)]
        pbt = sb("pbt", [P, HEADS * S])
        ao_inv = sb("ao_inv", [P, OCT * S])
        ao = sb("ao", [P, OCT, 2, S])
        r2 = sb("r2", [P, D])
        st2 = sb("st2", [P, 6])
        mv2 = sb("mv2", [P, 2])
        rstd2 = sb("rstd2", [P, 1])
        x2 = [sb(f"x2_{n}", [P, D]) for n in range(2)]
        x2t = sb("x2t", [P, P])
        logits = sb("logits", [P, NT, E])
        half_neg = sb("half_neg", [P, 1])
        ve1 = sb("ve1", [P, 1])
        ve2 = sb("ve2", [P, 1])

        tri_bf = sb("tri_bf", [P, P], BF16)
        ones_bf = sb("ones_bf", [P, P], BF16)
        lg_max = sb("lg_max", [P, NT])
        lg_exp = sb("lg_exp", [P, NT, E])
        lg_sub = sb("lg_sub", [P, NT, E])
        gate = sb("gate", [P, NT])
        gate_rest = sb("gate_rest", [P, NT])
        at_max = sb("at_max", [P, NT, E])
        first = sb("first", [P, NT])
        chosen = sb("chosen", [P, NT, E])
        chosen_bf = sb("chosen_bf", [P, NT, E], BF16)
        whole_i = sb("whole_i", [P, E], I32)
        ends = sb("ends", [P, E])
        starts = sb("starts", [P, E])
        place_e = sb("place_e", [P, NT, E])
        place_f = sb("place_f", [P, NT])
        place_i = sb("place_i", [P, NT], I32)
        lane_i = sb("lane_i", [P, NT], I32)
        tile_i = sb("tile_i", [P, NT], I32)
        tiles_e = sb("tiles_e", [P, E, E])
        lane_hot = sb("lane_hot", [P, NT, P], BF16)
        tile_hot = sb("tile_hot", [P, NT, FT], BF16)
        vals = sb("vals", [P, NT, VALS], BF16)
        tile_vals = sb("tile_vals", [P, NT, VALS, FT], BF16)
        sorted_sb = sb("sorted_sb", [P, VALS, FT])
        to_f = sb("to_f", [P, FT])
        from_row = sb("from_row", [P, FT], U32)
        to_row = sb("to_row", [P, FT], U32)
        gate_sum = sb("gate_sum", [P, FT])
        sorted_gate = sb("sorted_gate", [P, FT])
        past = sb("past", [P, FT, E])
        expert_f = sb("expert_f", [P, FT])
        expert_of = sb("expert_of", [P, FT], I32)

        near_sb = sb("near_sb", [P, E * NEAR])
        w2_cur = [sb(f"w2_cur{n}", [P, FB * D]) for n in range(2)]
        near = [sb(f"near{n}", [P, NEAR]) for n in range(2)]
        w2_sb = sb("w2_sb", [P, E * FB * D])
        from_cur = [sb(f"from_cur{n}", [P, 1], U32) for n in range(RING)]
        to_cur = [sb(f"to_cur{n}", [P, 1], U32) for n in range(RING)]
        xs = [sb(f"xs{n}", [P, D]) for n in range(RING)]
        xst = [sb(f"xst{n}", [P, P]) for n in range(2)]
        ht_sb = [sb(f"ht_sb{n}", [P, F]) for n in range(2)]
        xb = [sb(f"xb{n}", [P, D]) for n in range(2)]
        r3 = [sb(f"r3_{n}", [P, D]) for n in range(2)]
        st3 = sb("st3", [P, 6])
        mv3 = [sb(f"mv3_{n}", [P, 2]) for n in range(2)]
        ve3 = [sb(f"ve3_{n}", [P, 1]) for n in range(2)]
        rstd3 = [sb(f"rstd3_{n}", [P, 1]) for n in range(2)]
        res = [sb(f"res{n}", [P, D]) for n in range(RING)]

        ps_s = psum("ps_s", [P, BANK])
        ps_pt = psum("ps_pt", [P, BANK])
        ps_o = ps_pt[:, 0:D]
        ps_p = psum("ps_p", [P, BANK])
        ps_x1t = ps_p[:, 0:P]
        ps_x2t = ps_p[:, P:2 * P]
        ps_sc = psum("ps_sc", [P, 2 * BANK])
        ps_bt = psum("ps_bt", [P, 2 * BANK])
        ps_ov = ps_bt[:, 0:OCT * P]
        ps_os = ps_bt[:, OCT * P:OCT * (P + S)]
        ps_wo = ps_bt[:, 0:D]
        ps_vl = psum("ps_vl", [P, BANK])
        ps_v = ps_vl[:, 0:D]
        ps_log = ps_vl[:, D:D + E]
        ps_rank = ps_sc[:, 0:NT * E]
        ps_count = ps_sc[:, BANK:BANK + E]
        ps_sorted = ps_pt[:, 0:VALS * FT]
        ps_h = [ps_s[:, :], ps_pt[:, :]]
        ps_xs = ps_p[:, 0:P]
        ps_y = [ps_sc[:, 0:D], ps_sc[:, BANK:BANK + D]]

        consts_in = sem("consts_in")
        table_in = sem("table_in")
        keys_in = sem("keys_in")
        idle_set = sem("idle_set")
        proj_in = sem("proj_in")
        weights_in = sem("weights_in")
        pool_ones = sem("pool_ones")
        route = sem("route")
        shifted = sem("shifted")
        exp_ready = sem("exp_ready")
        chosen_ready = sem("chosen_ready")
        rank_ready = sem("rank_ready")
        hot_ready = sem("hot_ready")
        sorted_ready = sem("sorted_ready")
        gate_step = sem("gate_step")
        early_ranked = sem("early_ranked")
        vals_ready = sem("vals_ready")
        lane_ready = sem("lane_ready")
        tile_hot_ready = sem("tile_hot_ready")
        pool_vals_ready = sem("pool_vals_ready")
        expert_ready = sem("expert_ready")
        from_ready = sem("from_ready")
        xs_in = [sem(f"xs_in{n}") for n in range(RING)]
        from_copied = sem("from_copied")
        to_copied = sem("to_copied")
        xst_ready = sem("xst_ready")
        xst_copied = sem("xst_copied")
        h_ready = sem("h_ready")
        ht_copied = sem("ht_copied")
        y_ready = sem("y_ready")
        xb_ready = sem("xb_ready")
        near_copied = sem("near_copied")
        w2_copied = sem("w2_copied")
        r3_ready = sem("r3_ready")
        st3_ready = sem("st3_ready")
        var3_ready = sem("var3_ready")
        ve3_ready = sem("ve3_ready")
        rstd3_ready = sem("rstd3_ready")
        res_ready = sem("res_ready")
        out_stored = [sem(f"out_stored{n}") for n in range(RING)]
        x_in = [sem(f"x_in{n}") for n in range(2)]
        ctx_in = [sem(f"ctx_in{n}") for n in range(2)]
        s_ready = sem("s_ready")
        s_scaled = sem("s_scaled")
        nmax_ready = sem("nmax_ready")
        p_ready = sem("p_ready")
        pt_ready = sem("pt_ready")
        pt_copied = sem("pt_copied")
        o_ready = sem("o_ready")
        var1_ready = sem("var1_ready")
        ve1_ready = sem("ve1_ready")
        rstd1_ready = sem("rstd1_ready")
        x1_ready = sem("x1_ready")
        x1b_ready = sem("x1b_ready")
        x1t_ready = sem("x1t_ready")
        x1t_copied = sem("x1t_copied")
        v_ready = sem("v_ready")
        q_ready = sem("q_ready")
        v_copied = sem("v_copied")
        rope_ready = sem("rope_ready")
        qk_ready = sem("qk_ready")
        kbd_ready = sem("kbd_ready")
        sc_filled = sem("sc_filled")
        sc_half = sem("sc_half")
        sc_ready = sem("sc_ready")
        sc_masked = sem("sc_masked")
        scmax_ready = sem("scmax_ready")
        sd_ready = sem("sd_ready")
        pb_ready = sem("pb_ready")
        bt_ready = sem("bt_ready")
        bt_copied = sem("bt_copied")
        bo_ready = sem("bo_ready")
        ao_inv_ready = sem("ao_inv_ready")
        ao_ready = sem("ao_ready")
        wo_ready = sem("wo_ready")
        var2_ready = sem("var2_ready")
        ve2_ready = sem("ve2_ready")
        rstd2_ready = sem("rstd2_ready")
        x2_ready = sem("x2_ready")
        x2_stored = [sem(f"x2_stored{n}") for n in range(2)]
        x2t_ready = sem("x2t_ready")
        x2t_copied = sem("x2t_copied")
        log_ready = sem("log_ready")
        log_copied = sem("log_copied")
        setup_done = sem("setup_done")
        dve_passed = sem("dve_passed")
        pool_passed = sem("pool_passed")
        pool_setup = sem("pool_setup")
        pinv_ready = sem("pinv_ready")
        r1_ready = sem("r1_ready")
        st1_ready = sem("st1_ready")
        r2_ready = sem("r2_ready")
        st2_ready = sem("st2_ready")

        STAGES = 6

        def pipeline(eng, slot, looped=NT // 2):
            def run(group, place):
                def at(back):
                    t = Tile(group + (place - back) // 2, (place - back) % 2)
                    return None if isinstance(group, int) and not 0 <= t.index < NT else t
                slot(*(at(back) for back in range(STAGES)))

            for s in range(STAGES):
                run(s // 2, s % 2)
            with eng.Fori(STAGES // 2, looped) as g:
                run(g, 0)
                run(g, 1)
            for s in range(2 * looped, NT + STAGES - 1):
                run(s // 2, s % 2)

        def expert_pipeline(eng, slot):
            def at(s, back):
                group, place = s[0] + (s[1] - back) // RING, (s[1] - back) % RING
                t = Tile(group, place, RING)
                return None if isinstance(group, int) and not 0 <= t.index < FT else t

            def run(s):
                slot(at(s, 0), at(s, 1), at(s, 2), at(s, 3), at(s, -2))

            ahead = RING + 3
            looped = (FT - 2 - ahead) // RING
            for s in range(ahead):
                run((s // RING, s % RING))
            with eng.Fori(1, 1 + looped) as g:
                for n in range(3, RING + 3):
                    run((g + n // RING, n % RING))
            for s in range(ahead + looped * RING, FT + 3):
                run((s // RING, s % RING))

        block = ctx.enter_context(nc.Block())

        @block.sync
        def _(sp):
            def load(dst, src, done):
                sp.dma_start(dst, src).then_inc(done, 16)

            def load_first(a):
                wait_before(sp, s_ready, a, 2)
                wait_before(sp, s_scaled, a, 2)
                wait_before(sp, r1_ready, a, 2)
                load(xt[a.place][:, :], x_t[:, bass.ts(a.index, P)], x_in[a.place])
                load(xk[a.place][:, :], x_tok[bass.ts(a.index, P), :], x_in[a.place])
                for n in range(2):
                    load(scale_bc[a.place][n * S:(n + 1) * S, :],
                         x_scale[bass.ds(a.index * 2 + n, 1), :].to_broadcast([S, T]), x_in[a.place])

            def load_expert(e):
                cols = e * NEAR
                load(near_sb[:, cols:cols + F], w1[:, bass.ts(e, F)], weights_in)
                load(near_sb[:, cols + F:cols + F + FB], b1[:, bass.ts(e, FB)], weights_in)
                load(near_sb[:, cols + F + FB:cols + NEAR], b2[:, bass.ts(e, D)].to_broadcast([P, D]), weights_in)
                load(w2_sb[:, bass.ts(e, FB * D)], w2[:, bass.ts(e, FB * D)], weights_in)

            def slot(a, p, q, r, w, c):
                if a:
                    after = Tile(a.group + (a.place + 1) // 2, 1 - a.place)
                    if not isinstance(after.index, int) or after.index < NT:
                        load_first(after)
                    wait_before(sp, v_ready, a, 2)
                    wait_before(sp, sc_masked, a, 2)
                    load(ct[a.place][:, :], ctx_t[:, bass.ts(a.index, P)], ctx_in[a.place])
                    load(mk[a.place][:, :], mask[bass.ts(a.index, P), :], ctx_in[a.place])
                    if isinstance(a.index, int) and a.index == 0:
                        for dst, src in ((w_qk[:, 0, :], wq), (w_qk[:, 1, :], wk), (w_qk[:, 2, :], wq_swap),
                                         (w_qk[:, 3, :], wk_swap), (w_v[:, :, :].rearrange("p n c -> p (n c)"), wv),
                                         (w_o[:, :, :, :].rearrange("p n g d -> p (n g d)"), wo),
                                         (bo_bc[:, :], bo.to_broadcast([P, D])), (r_w[:, :], router_w),
                                         (r_b[:, :], router_b.to_broadcast([P, E]))):
                            load(dst, src, proj_in)
                    if isinstance(a.index, int) and 2 <= a.index < STAGES:
                        for e in range(2 * (a.index - 2), 2 * (a.index - 1)):
                            load_expert(e)
                if w:
                    sp.wait_ge(x2_ready, w.done)
                    sp.dma_start(x2_dram[bass.ts(w.index, P), :], x2[w.place][:, :]).then_inc(x2_stored[w.place], 16)

            load(kt_sb[:, :], attn_kt, keys_in)
            load_first(Tile(0, 0))
            load(ident, consts[:, C_ID:C_ID + P], consts_in)
            load(v_sb[:, :, :], attn_v, consts_in)
            load(cst[:, C_COS:], consts[:, C_COS:], consts_in)
            pipeline(sp, slot, NT // 2 - 1)

        CONSTS = 3 * 16
        PROJ = 9 * 16
        WEIGHTS = E * 4 * 16

        @block.tensor
        def _(pe):
            def keep_warm(count, into):
                for _ in range(count):
                    nc.tensor.matmul(into, idle_sb[:, 0:P], idle_sb[:, :], start=True, stop=True)

            def score_rows(q, groups):
                for g in groups:
                    rows = slice(g * 32, g * 32 + 32)
                    col = (g % 2) * BANK + (g // 2) * GROUP_KEYS
                    for n in range(2):
                        mm = nc.tensor.matmul(ps_sc[n * S:(n + 1) * S, col:col + GROUP_KEYS],
                                              qkt[q.place][rows, n * S:(n + 1) * S],
                                              kbd[q.place][rows, n].rearrange("p h k -> p (h k)"),
                                              start=True, stop=True, tile_position=(g * 32, n * S))
                return mm

            def rank(lo, hi):
                pe.wait_ge(chosen_ready, 2 if lo else 1)
                hot = chosen_bf[:, :, :].rearrange("p t e -> p (t e)")
                nc.tensor.matmul(ps_rank[:, lo * E:], tri_bf[:, :], hot[:, lo * E:], start=(lo == 0), stop=False)
                for t in range(1, NT - lo):
                    nc.tensor.matmul(ps_rank[:, (lo + t) * E:], ones_bf[:, :], hot[:, lo * E:(NT - t) * E], start=False,
                                     stop=(hi == NT and t == NT - lo - 1))
                for t in range(lo, hi):
                    mm = nc.tensor.matmul(ps_count, ones_bf[:, :], hot[:, t * E:(t + 1) * E], start=(t == 0),
                                          stop=(t == NT - 1))
                mm.then_inc(rank_ready if lo else early_ranked, 1)

            def slot(a, p, q, r, w, c):
                if c and isinstance(c.index, int) and c.index == NT_EARLY:
                    pe.wait_ge(sc_masked, NT)
                    pe.wait_ge(pool_ones, 1)
                    pe.wait_ge(setup_done, 4)
                    rank(0, NT_EARLY)
                if not a and r:
                    pe.wait_ge(s_scaled, NT)
                    keep_warm(1, ps_s[:, :])
                if a:
                    pe.wait_ge(x_in[a.place], (a.group + 1) * 64)
                    wait_before(pe, s_scaled, a)
                    nc.tensor.matmul(ps_s[:, :], xt[a.place][:, :], kt_sb[:, :], start=True,
                                     stop=True).then_inc(s_ready, 1)
                    if isinstance(a.index, int) and a.index < 2:
                        keep_warm(1, ps_bt[:, 0:BANK])
                if q:
                    pe.wait_ge(kbd_ready, q.index * 2 + 2)
                    wait_before(pe, sc_masked, q)
                    score_rows(q, (0, 1)).then_inc(sc_half, 1)
                if p:
                    pe.wait_ge(x1_ready, p.done)
                    wait_before(pe, rope_ready, p)
                    if c:
                        wait_before(pe, x2t_copied, c)
                    nc.tensor.transpose(ps_x1t, x1[p.place][:, :], ident).then_inc(x1t_ready, 1)
                if c:
                    pe.wait_ge(x2_ready, c.done)
                    if not p:
                        pe.wait_ge(rope_ready, NT)
                        wait_before(pe, x2t_copied, c)
                    nc.tensor.transpose(ps_x2t, x2[c.place][:, :], ident).then_inc(x2t_ready, 1)
                if q:
                    if isinstance(q.index, int) and q.index == 0:
                        pe.wait_ge(proj_in, PROJ)
                    pe.wait_ge(ctx_in[q.place], (q.group + 1) * 32)
                    wait_before(pe, v_copied, q)
                    if c:
                        wait_before(pe, log_copied, c)
                    for n in range(2):
                        for m in range(2):
                            mm = nc.tensor.matmul(ps_v[m * S:(m + 1) * S, n * (D // 2):(n + 1) * (D // 2)],
                                                  ct[q.place][:, n * S:(n + 1) * S], w_v[:, m, :], start=True,
                                                  stop=True, tile_position=(0, m * S))
                    mm.then_inc(v_ready, 1)
                if w:
                    pe.wait_ge(ao_ready, w.done)
                    for g in range(OCT):
                        for n in range(2):
                            mm = nc.tensor.matmul(ps_wo[n * S:(n + 1) * S, :],
                                                  ao[:, g, n, :], w_o[:, n, g, :],
                                                  start=(g == 0), stop=(g == OCT - 1), tile_position=(0, n * S))
                    mm.then_inc(wo_ready, 1)
                if c:
                    pe.wait_ge(x2t_copied, c.done)
                    if not q:
                        pe.wait_ge(v_copied, NT)
                        wait_before(pe, log_copied, c)
                    nc.tensor.matmul(ps_log, x2t[:, :], r_w[:, :], start=True, stop=True).then_inc(log_ready, 1)
                if q:
                    pe.wait_ge(sc_half, q.done)
                    score_rows(q, (2, 3)).then_inc(sc_ready, 1)
                if p:
                    if isinstance(p.index, int) and p.index == 0:
                        pe.wait_ge(proj_in, PROJ)
                    pe.wait_ge(ctx_in[p.place], (p.group + 1) * 32)
                    pe.wait_ge(x1t_copied, p.done)
                    if c:
                        pe.wait_ge(x2t_copied, c.done)
                    for n in range(2):
                        nc.tensor.matmul(ps_p[:, (2 * n + 1) * P:(2 * n + 2) * P], w_qk[:, 2 * n + 1, :],
                                         ct[p.place][:, :], start=True, stop=True)
                        mm = nc.tensor.matmul(ps_p[:, 2 * n * P:(2 * n + 1) * P], w_qk[:, 2 * n, :], x1t[:, :],
                                              start=True, stop=True)
                    mm.then_inc(q_ready, 1)
                if a:
                    if isinstance(a.index, int) and a.index == 0:
                        pe.wait_ge(consts_in, CONSTS)
                    pe.wait_ge(p_ready, a.done)
                    wait_before(pe, r1_ready, a)
                    for t in range(TB):
                        mm = nc.tensor.transpose(ps_pt[:, t * P:(t + 1) * P], p_sb[:, t * P:(t + 1) * P], ident)
                    mm.then_inc(pt_ready, 1)
                if r:
                    pe.wait_ge(pb_ready, r.done)
                    if w:
                        pe.wait_ge(r2_ready, w.done)
                    for h in range(HPAIR):
                        mm = nc.tensor.transpose(ps_bt[:, h * P:(h + 1) * P], pb_sb[r.place][:, h * P:(h + 1) * P],
                                                 ident)
                        if h % (HPAIR // 2) == HPAIR // 2 - 1:
                            mm.then_inc(bt_ready, 1)
                if a:
                    pe.wait_ge(pt_copied, a.done)
                    for t in range(TB):
                        mm = nc.tensor.matmul(ps_o, pt_sb[:, t * P:(t + 1) * P], v_sb[:, t, :], start=(t == 0),
                                              stop=(t == TB - 1))
                    mm.then_inc(o_ready, 1)
                if r:
                    for g in range(OCT):
                        pe.wait_ge(bt_copied, r.index * 2 + (1 + g))
                        for j in range(CG):
                            h = g * CG + j
                            nc.tensor.matmul(ps_ov[j * 32:(j + 1) * 32, g * P:(g + 1) * P],
                                             vz[r.place][:, h].rearrange("p n c -> p (n c)"),
                                             pbt[:, h * P:(h + 1) * P], start=True, stop=True,
                                             tile_position=(0, j * 32))
                        for n in range(2):
                            for j in range(CG):
                                h = g * CG + j
                                mm = nc.tensor.matmul(ps_os[j * 32:(j + 1) * 32, g * S:(g + 1) * S],
                                                      own_keys[:, n].rearrange("p m c -> p (m c)"),
                                                      pbt[:, h * P + n * S:h * P + (n + 1) * S], start=(n == 0),
                                                      stop=(n == 1), tile_position=(0, j * 32))
                    mm.then_inc(bo_ready, 1)

            def expert_slot(x, h, y, done, ahead):
                if x:
                    pe.wait_ge(xs_in[x.place], x.landed)
                    wait_before(pe, xst_copied, x)
                    nc.tensor.transpose(ps_xs, xs[x.place][:, :], ident).then_inc(xst_ready, 1)
                if h:
                    pe.wait_ge(near_copied, h.done)
                    pe.wait_ge(xst_copied, h.done)
                    wait_before(pe, ht_copied, h, 2)
                    for f in range(FB):
                        mm = nc.tensor.matmul(ps_h[h.place % 2][:, f * P:(f + 1) * P],
                                              near[h.place % 2][:, f * P:(f + 1) * P], xst[h.place % 2][:, :],
                                              start=True, stop=True)
                    mm.then_inc(h_ready, 1)
                if y:
                    pe.wait_ge(ht_copied, y.done)
                    pe.wait_ge(w2_copied, y.done)
                    wait_before(pe, r3_ready, y, 2)
                    for f in range(FB):
                        mm = nc.tensor.matmul(ps_y[y.place % 2], ht_sb[y.place % 2][:, f * P:(f + 1) * P],
                                              w2_cur[y.place % 2][:, f * D:(f + 1) * D], start=(f == 0),
                                              stop=(f == FB - 1))
                    mm.then_inc(y_ready, 1)

            pe.wait_ge(idle_set, 1)
            keep_warm(2, ps_bt[:, 0:BANK])
            pe.wait_ge(keys_in, 16)
            pipeline(pe, slot)

            rank(NT_EARLY, NT)
            pe.wait_ge(hot_ready, 1)
            pe.wait_ge(pool_vals_ready, 1)
            for t in range(NT):
                if t == POOL_VALS:
                    pe.wait_ge(hot_ready, 2)
                mm = nc.tensor.matmul(ps_sorted, lane_hot[:, t, :],
                                      tile_vals[:, t].rearrange("p v j -> p (v j)"), start=(t == 0), stop=(t == NT - 1))
            mm.then_inc(sorted_ready, 1)
            keep_warm(3, ps_s[:, :])
            expert_pipeline(pe, expert_slot)

        @block.scalar
        def _(act):
            def slot(a, p, q, r, w, c):
                if p:
                    act.wait_ge(x1t_ready, p.done)
                    if c:
                        act.wait_ge(x2t_ready, c.done)
                    wait_before(act, q_ready, p)
                    nc.scalar.copy(x1t[:, :], ps_x1t).then_inc(x1t_copied, 1)
                if c:
                    act.wait_ge(x2t_ready, c.done)
                    wait_before(act, log_ready, c)
                    nc.scalar.copy(x2t[:, :], ps_x2t).then_inc(x2t_copied, 1)
                if a:
                    act.wait_ge(nmax_ready, a.done)
                    wait_before(act, pt_ready, a)
                    wait_before(act, pinv_ready, a)
                    nc.scalar.activation(p_sb[:, :], s_sb[:, :], ACT.Exp, bias=s_nmax[:, :],
                                         accum_out=p_sum[:, :]).then_inc(p_ready, 1)
                if r:
                    act.wait_ge(sd_ready, r.done)
                    nc.scalar.activation(pb_sb[r.place][:, :], sd_sb[:, :, :].rearrange("p h k -> p (h k)"),
                                         ACT.Exp).then_inc(pb_ready, 1)
                if a:
                    act.wait_ge(pt_ready, a.done)
                    wait_before(act, o_ready, a)
                    nc.scalar.copy(pt_sb[:, :], ps_pt[:, :]).then_inc(pt_copied, 1)
                if r:
                    for n in range(2):
                        act.wait_ge(bt_ready, r.index * 2 + (1 + n))
                        if n == 0:
                            wait_before(act, bo_ready, r)
                        nc.scalar.copy(pbt[:, n * BANK:(n + 1) * BANK],
                                       ps_bt[:, n * BANK:(n + 1) * BANK]).then_inc(bt_copied, 1)
                if q:
                    if isinstance(q.index, int) and q.index == 0:
                        act.wait_ge(setup_done, 4)
                    act.wait_ge(v_ready, q.done)
                    if c:
                        act.wait_ge(log_copied, c.done)
                    wait_before(act, bo_ready, q, 2)
                    for n in range(2):
                        rows = slice(n * S, (n + 1) * S)
                        cp = nc.scalar.copy(vz[q.place][rows, :, :, n * HD:(n + 1) * HD],
                                            ps_v[rows, :].rearrange("p (m g d) -> p g m d", m=2, d=HD))
                    cp.then_inc(v_copied, 1)
                if p:
                    if isinstance(p.index, int) and p.index == 0:
                        act.wait_ge(consts_in, CONSTS)
                    act.wait_ge(qk_ready, p.done)
                    wait_before(act, sc_ready, p, 2)
                    for h in range(HG):
                        mm = nc.scalar.activation(kbd[p.place][:, :, h, :],
                                                  qkt[p.place][:, P:2 * P].rearrange("p (n k) -> p n k", n=2),
                                                  ACT.Copy, scale=cst[:, C_HM + h:C_HM + h + 1])
                        if h % 2 == 1:
                            mm.then_inc(kbd_ready, 1)

            def name_rows(j):
                nc.scalar.copy(from_cur[j.place][:, :], from_row[:, bass.ds(j.index, 1)]).then_inc(from_copied, 1)

            def expert_slot(x, h, y, done, ahead):
                if ahead and not (isinstance(ahead.index, int) and ahead.index < RING):
                    act.wait_ge(xs_in[ahead.place], ahead.group * 16)
                    name_rows(ahead)
                if x:
                    expert = act.value_load(expert_of[0:1, bass.ds(x.index, 1)], min_val=0, max_val=E - 1)
                    wait_before(act, h_ready, x, 2)
                    wait_before(act, ht_copied, x, 2)
                    wait_before(act, xb_ready, x, 2)
                    nc.scalar.copy(near[x.place % 2][:, :], near_sb[:, bass.ts(expert, NEAR)]
                                   ).then_inc(near_copied, 1)
                if x:
                    act.wait_ge(xst_ready, x.done)
                    wait_before(act, h_ready, x, 2)
                    nc.scalar.copy(xst[x.place % 2][:, :], ps_xs).then_inc(xst_copied, 1)
                if h:
                    act.wait_ge(h_ready, h.done)
                    wait_before(act, y_ready, h, 2)
                    for f in range(FB):
                        cols = slice(f * P, (f + 1) * P)
                        relu = nc.scalar.activation(ht_sb[h.place % 2][:, cols], ps_h[h.place % 2][:, cols], ACT.Relu,
                                                    bias=near[h.place % 2][:, F + f:F + f + 1])
                    relu.then_inc(ht_copied, 1)
                if done:
                    if not (isinstance(done.group, int) and done.group == 0):
                        act.wait_ge(out_stored[done.place], done.group * 16)
                    nc.scalar.copy(to_cur[done.place][:, :], to_row[:, bass.ds(done.index, 1)]).then_inc(to_copied, 1)

            act.wait_ge(pool_setup, 1)
            nc.scalar.activation(rstd1[:, :], half_neg[:, :], ACT.Exp).then_inc(table_in, 1)
            pipeline(act, slot)
            act.wait_ge(shifted, 1)
            nc.scalar.activation(lg_exp[:, :, :].rearrange("p t e -> p (t e)"),
                                 lg_sub[:, :, :].rearrange("p t e -> p (t e)"), ACT.Exp).then_inc(exp_ready, 1)
            act.wait_ge(from_ready, 1)
            for n in range(RING):
                name_rows(Tile(0, n, RING))
            act.wait_ge(expert_ready, 1)
            act.wait_ge(weights_in, WEIGHTS)
            expert_pipeline(act, expert_slot)

        @block.vector
        def _(dve):
            def moments(r, stats, mv, stats_done, var_ready, tile):
                nc.vector.bn_stats(stats[:, :], r[:, :]).then_inc(stats_done, 1)
                dve.wait_ge(stats_done, tile.done)
                carry(dve, dve_passed)
                nc.vector.bn_aggr(mv[:, :], stats[:, :]).then_inc(var_ready, 1)

            def slot(a, p, q, r, w, c):
                if a:
                    dve.wait_ge(s_ready, a.done)
                    dve.wait_ge(x_in[a.place], (a.group + 1) * 64)
                    wait_before(dve, p_ready, a)
                    carry(dve, dve_passed)
                    nc.vector.tensor_tensor_reduce(out=s_sb[:, :], in0=ps_s[:, :], in1=scale_bc[a.place][:, :],
                                                   scale=1.0, scalar=-3.0e38, op0=ALU.mult, op1=ALU.max,
                                                   accum_out=s_max[:, :]).then_inc(s_scaled, 1)
                    dve.wait_ge(s_scaled, a.done)
                    nc.vector.tensor_scalar(s_nmax[:, :], s_max[:, :], -1.0, None, ALU.mult).then_inc(nmax_ready, 1)
                if q and isinstance(q.index, int) and q.index == 0:
                    dve.wait_ge(consts_in, CONSTS)
                    for n in range(2):
                        cp = nc.vector.memset(vz[n][:, :, :, :], 0.0)
                    cp.then_inc(setup_done, 1)
                    nc.vector.tensor_copy(vals[:, :, 0:2], cst[:, C_TOK:C_TOK + 2 * NT].rearrange(
                        "p (t v) -> p t v", v=2)).then_inc(setup_done, 1)
                    nc.vector.tensor_copy(tri_bf[:, :], cst[:, C_TRI:C_TRI + P]).then_inc(setup_done, 1)
                    nc.vector.memset(chosen_bf[:, NT_EARLY:, :], 0.0).then_inc(setup_done, 1)
                    dve.wait_ge(setup_done, 4)
                if w:
                    dve.wait_ge(wo_ready, w.done)
                    nc.vector.tensor_tensor(r2[:, :], ps_wo, x1b[:, bass.ts(w.index, D)], ALU.add).then_inc(r2_ready, 1)
                    dve.wait_ge(r2_ready, w.done)
                    moments(r2, st2, mv2, st2_ready, var2_ready, w)
                if q:
                    dve.wait_ge(sc_ready, q.done)
                    dve.wait_ge(sc_filled, q.done)
                    dve.wait_ge(ctx_in[q.place], (q.group + 1) * 32)
                    carry(dve, dve_passed)
                    for n in range(2):
                        keep = mk[q.place][:, :].unsqueeze(1).unsqueeze(1).to_broadcast([P, 2, HG, S])
                        into = sc_sb[:, :, :].rearrange("p (m n h) k -> p n m h k", m=2, n=2)[:, n]
                        cp = nc.vector.copy_predicated(
                            into, keep, ps_sc[:, n * BANK:(n + 1) * BANK].rearrange("p (m h k) -> p m h k", m=2, k=S))
                    cp.then_inc(sc_masked, 1)
                if c:
                    if isinstance(c.index, int) and c.index == 0:
                        dve.wait_ge(proj_in, PROJ)
                    dve.wait_ge(log_ready, c.done)
                    nc.vector.tensor_tensor(logits[:, bass.ds(c.index, 1), :].rearrange("p t e -> p (t e)"), ps_log,
                                            r_b[:, :], ALU.add).then_inc(log_copied, 1)
                if p:
                    if isinstance(p.index, int) and p.index == 0:
                        dve.wait_ge(consts_in, CONSTS)
                    dve.wait_ge(q_ready, p.done)
                    wait_before(dve, qk_ready, p)
                    nc.vector.tensor_tensor(rope_c[:, :], ps_p[:, 0:2 * P], cst[:, C_COS:C_COS + 2 * P], ALU.mult)
                    nc.vector.tensor_tensor(rope_s[:, :], ps_p[:, 2 * P:4 * P], cst[:, C_SIN:C_SIN + 2 * P],
                                            ALU.mult).then_inc(rope_ready, 1)
                if w:
                    if not (isinstance(w.group, int) and w.group == 0):
                        dve.wait_ge(x2_stored[w.place], w.group * 16)
                    wait_before(dve, x2t_ready, w, 2)
                    dve.wait_ge(rstd2_ready, w.done)
                    nc.vector.tensor_scalar(x2[w.place][:, :], r2[:, :], mv2[:, 0:1], rstd2[:, 0:1], ALU.subtract,
                                            ALU.mult).then_inc(x2_ready, 1)
                if q:
                    dve.wait_ge(sc_masked, q.done)
                    wait_before(dve, sd_ready, q)
                    nc.vector.tensor_reduce(sc_max[:, :], sc_sb[:, :, :], AX.X, ALU.max).then_inc(scmax_ready, 1)
                if a:
                    dve.wait_ge(p_ready, a.done)
                    nc.vector.reciprocal(p_inv[:, :], p_sum[:, :]).then_inc(pinv_ready, 1)
                    dve.wait_ge(pinv_ready, a.done)
                    dve.wait_ge(o_ready, a.done)
                    nc.vector.scalar_tensor_tensor(out=r1[:, :], in0=ps_o, scalar=p_inv[:, 0:1],
                                                   in1=xk[a.place][:, :], op0=ALU.mult, op1=ALU.add).then_inc(r1_ready, 1)
                    dve.wait_ge(r1_ready, a.done)
                    moments(r1, st1, mv1, st1_ready, var1_ready, a)
                if c and isinstance(c.index, int) and c.index == NT_EARLY - 1:
                    dve.wait_ge(log_copied, NT_EARLY)
                    choose(0, NT_EARLY)
                if r:
                    dve.wait_ge(bo_ready, r.done)
                    wait_before(dve, wo_ready, r)
                    nc.vector.reciprocal(ao_inv[:, :], ps_os).then_inc(ao_inv_ready, 1)
                if a:
                    wait_before(dve, x1t_ready, a, 2)
                    wait_before(dve, x1b_ready, a, 2)
                    dve.wait_ge(rstd1_ready, a.done)
                    nc.vector.tensor_scalar(x1[a.place][:, :], r1[:, :], mv1[:, 0:1], rstd1[:, 0:1], ALU.subtract,
                                            ALU.mult).then_inc(x1_ready, 1)
                if r:
                    dve.wait_ge(ao_inv_ready, r.done)
                    nc.vector.tensor_tensor(ao[:, :, :, :], ps_ov.rearrange("p (g n t) -> p g n t", g=OCT, n=2),
                                            spread(ao_inv[:, :].rearrange("p (g t) -> p g t", g=OCT), 2,
                                                   [P, OCT, 2, S]), ALU.mult).then_inc(ao_ready, 1)

            class Chain:

                def __init__(self, done):
                    self.done, self.count = done, 0

                def previous(self):
                    dve.wait_ge(self.done, self.count)

                def add(self, ins):
                    self.count += 1
                    ins.then_inc(self.done, 1)

                def then(self, ins):
                    self.add(ins)
                    self.previous()

            v = nc.vector
            main, gates = Chain(route), Chain(gate_step)

            def choose(lo, hi):
                n = hi - lo
                weight8 = spread(cst[:, C_W8:C_W8 + E], 1, [P, n, E])
                main.then(v.tensor_reduce(lg_max[:, lo:hi], logits[:, lo:hi, :], AX.X, ALU.max))
                main.then(v.tensor_tensor(at_max[:, lo:hi, :], logits[:, lo:hi, :],
                                          spread(lg_max[:, lo:hi], 2, [P, n, E]), ALU.is_ge))
                main.then(v.tensor_tensor(chosen[:, lo:hi, :], at_max[:, lo:hi, :], weight8, ALU.mult))
                main.then(v.tensor_reduce(first[:, lo:hi], chosen[:, lo:hi, :], AX.X, ALU.max))
                main.then(v.tensor_tensor(chosen[:, lo:hi, :], weight8, spread(first[:, lo:hi], 2, [P, n, E]),
                                          ALU.is_equal))
                if lo:
                    dve.wait_ge(early_ranked, 1)
                v.tensor_copy(chosen_bf[:, lo:hi, :], chosen[:, lo:hi, :]).then_inc(chosen_ready, 1)

            def routing():
                before = cst[:, C_LT:C_LT + E * E].rearrange("p (e b) -> p e b", b=E)
                upto = cst[:, C_LE:C_LE + E * E].rearrange("p (e b) -> p e b", b=E)
                then = main.then
                dve.wait_ge(log_copied, NT)
                choose(NT_EARLY, NT)
                v.tensor_tensor(lg_sub[:, :, :], logits[:, :, :], spread(lg_max[:, :], 2, [P, NT, E]),
                                ALU.subtract).then_inc(shifted, 1)
                dve.wait_ge(rank_ready, 1)
                then(v.tensor_scalar(whole_i[:, :], ps_count, float(P - 1), None, ALU.add))
                then(v.tensor_scalar(whole_i[:, :], whole_i[:, :], 7, None, ALU.arith_shift_right))
                then(v.tensor_tensor(tiles_e[:, :, :], spread(whole_i[:, :], 1, [P, E, E]), before, ALU.mult))
                main.add(v.tensor_reduce(starts[:, :], tiles_e[:, :, :], AX.X, ALU.add))
                dve.wait_ge(exp_ready, 1)
                gates.add(v.tensor_reduce(first[:, :], lg_exp[:, :, :], AX.X, ALU.add))
                main.previous()
                main.add(v.tensor_tensor(place_e[:, :, :], ps_rank.rearrange("p (t e) -> p t e", e=E),
                                         spread(starts[:, :], 1, [P, NT, E]), ALU.add))
                gates.previous()
                gates.add(v.reciprocal(gate[:, :], first[:, :]))
                main.previous()
                main.add(v.tensor_tensor(place_e[:, :, :], place_e[:, :, :], chosen[:, :, :], ALU.mult))
                gates.previous()
                gates.add(v.tensor_copy(vals[:, :, 2], gate[:, :]))
                main.previous()
                main.then(v.tensor_reduce(place_f[:, :], place_e[:, :, :], AX.X, ALU.add))
                main.add(v.tensor_copy(place_i[:, :], place_f[:, :]))
                gates.previous()
                gates.add(v.tensor_tensor(gate_rest[:, :], gate[:, :], vals[:, :, 2], ALU.subtract))
                main.previous()
                v.tensor_scalar(lane_i[:, :], place_i[:, :], P - 1, None, ALU.bitwise_and).then_inc(lane_ready, 1)
                main.add(v.tensor_scalar(tile_i[:, :], place_i[:, :], 7, None, ALU.arith_shift_right))
                gates.previous()
                gates.add(v.tensor_copy(vals[:, :, 3], gate_rest[:, :]))
                main.previous()
                v.tensor_tensor(tile_hot[:, :, :], spread(cst[:, C_IOTA:C_IOTA + FT], 1, [P, NT, FT]),
                                spread(tile_i[:, :], 2, [P, NT, FT]), ALU.is_equal).then_inc(tile_hot_ready, 1)
                gates.previous()
                v.tensor_tensor(vals[:, :, 4], gate_rest[:, :], vals[:, :, 3], ALU.subtract).then_inc(vals_ready, 1)
                dve.wait_ge(lane_ready, 1)
                v.tensor_tensor(lane_hot[:, :, :], spread(cst[:, C_IOTA:C_IOTA + P], 1, [P, NT, P]),
                                spread(lane_i[:, :], 2, [P, NT, P]), ALU.is_equal).then_inc(hot_ready, 1)
                dve.wait_ge(tile_hot_ready, 1)
                dve.wait_ge(vals_ready, 1)
                rest = NT - POOL_VALS
                v.tensor_tensor(tile_vals[:, POOL_VALS:], spread(tile_hot[:, POOL_VALS:, :], 2, [P, rest, VALS, FT]),
                                spread(vals[:, POOL_VALS:, :], 3, [P, rest, VALS, FT]), ALU.mult).then_inc(hot_ready, 1)
                then(v.tensor_tensor(tiles_e[:, :, :], spread(whole_i[:, :], 1, [P, E, E]), upto, ALU.mult))
                then(v.tensor_reduce(ends[:, :], tiles_e[:, :, :], AX.X, ALU.add))
                then(v.tensor_tensor(past[:, :, :], spread(cst[:, C_IOTA:C_IOTA + FT], 2, [P, FT, E]),
                                     spread(ends[:, :], 1, [P, FT, E]), ALU.is_ge))
                dve.wait_ge(sorted_ready, 1)
                then(v.tensor_copy(sorted_sb[:, :, :].rearrange("p v j -> p (v j)"), ps_sorted))
                v.scalar_tensor_tensor(out=from_row[:, :], in0=sorted_sb[:, 0, :], scalar=float(P),
                                       in1=sorted_sb[:, 1, :], op0=ALU.mult, op1=ALU.add).then_inc(from_ready, 1)
                then(v.tensor_reduce(expert_f[:, :], past[:, :, :], AX.X, ALU.add))
                v.tensor_scalar(expert_of[:, :], expert_f[:, :], float(E - 1), None,
                                ALU.min).then_inc(expert_ready, 1)
                v.tensor_scalar(to_f[:, :], sorted_sb[:, 2, :], 0.0, float(2 * NT * P), ALU.is_equal, ALU.mult)
                then(v.tensor_tensor(gate_sum[:, :], sorted_sb[:, 3, :], sorted_sb[:, 4, :], ALU.add))
                dve.wait_ge(from_ready, 1)
                then(v.tensor_tensor(to_row[:, :], to_f[:, :], from_row[:, :], ALU.add))
                then(v.tensor_tensor(sorted_gate[:, :], sorted_sb[:, 2, :], gate_sum[:, :], ALU.add))

            def expert_slot(x, h, y, done, ahead):
                if h:
                    expert = dve.value_load(expert_of[0:1, bass.ds(h.index, 1)], min_val=0, max_val=E - 1)
                    wait_before(dve, y_ready, h, 2)
                    nc.vector.tensor_copy(w2_cur[h.place % 2][:, :], w2_sb[:, bass.ts(expert, FB * D)]
                                          ).then_inc(w2_copied, 1)
                if h:
                    dve.wait_ge(near_copied, h.done)
                    dve.wait_ge(xs_in[h.place], h.landed)
                    wait_before(dve, r3_ready, h, 2)
                    nc.vector.scalar_tensor_tensor(out=xb[h.place % 2][:, :], in0=near[h.place % 2][:, F + FB:],
                                                   scalar=sorted_gate[:, bass.ds(h.index, 1)], in1=xs[h.place][:, :],
                                                   op0=ALU.mult, op1=ALU.add).then_inc(xb_ready, 1)
                if y:
                    dve.wait_ge(xb_ready, y.done)
                    dve.wait_ge(y_ready, y.done)
                    wait_before(dve, res_ready, y, 2)
                    nc.vector.scalar_tensor_tensor(out=r3[y.place % 2][:, :], in0=ps_y[y.place % 2],
                                                   scalar=sorted_gate[:, bass.ds(y.index, 1)], in1=xb[y.place % 2][:, :],
                                                   op0=ALU.mult, op1=ALU.add).then_inc(r3_ready, 1)
                    dve.wait_ge(r3_ready, y.done)
                    nc.vector.bn_stats(st3[:, :], r3[y.place % 2][:, :]).then_inc(st3_ready, 1)
                if done:
                    dve.wait_ge(rstd3_ready, done.done)
                    if not (isinstance(done.group, int) and done.group == 0):
                        dve.wait_ge(out_stored[done.place], done.group * 16)
                    nc.vector.tensor_scalar(res[done.place][:, :], r3[done.place % 2][:, :],
                                            mv3[done.place % 2][:, 0:1], rstd3[done.place % 2][:, 0:1], ALU.subtract,
                                            ALU.mult).then_inc(res_ready, 1)
                if y:
                    dve.wait_ge(st3_ready, y.done)
                    carry(dve, dve_passed)
                    nc.vector.bn_aggr(mv3[y.place % 2][:, :], st3[:, :]).then_inc(var3_ready, 1)
                    dve.wait_ge(var3_ready, y.done)
                    nc.vector.tensor_scalar(ve3[y.place % 2][:, :], mv3[y.place % 2][:, 1:2], EPS, None,
                                            ALU.add).then_inc(ve3_ready, 1)

            nc.vector.memset(idle_sb[:, :], 0.0).then_inc(idle_set, 1)
            pipeline(dve, slot)
            routing()
            dve.wait_ge(weights_in, WEIGHTS)
            dve.wait_ge(expert_ready, 1)
            expert_pipeline(dve, expert_slot)

        @block.gpsimd
        def _(pool):
            def root(var, ve, ready_var, ve_ready, rstd, rstd_ready, tile):
                pool.wait_ge(ready_var, tile.done)
                carry(pool, pool_passed)
                nc.gpsimd.tensor_scalar(ve[:, :], var, EPS, 1.0, ALU.add, ALU.mult).then_inc(ve_ready, 1)
                pool.wait_ge(ve_ready, tile.done)
                nc.gpsimd.tensor_tensor(rstd[:, :], ve[:, :], half_neg[:, :], ALU.pow).then_inc(rstd_ready, 1)

            def slot(a, p, q, r, w, c):
                if q:
                    wait_before(pool, sd_ready, q)
                    carry(pool, pool_passed)
                    nc.gpsimd.memset(sc_sb[:, :, :], MASKED).then_inc(sc_filled, 1)
                if p:
                    if isinstance(p.index, int) and p.index == 0:
                        pool.wait_ge(proj_in, PROJ)
                    pool.wait_ge(x1_ready, p.done)
                    nc.gpsimd.tensor_tensor(x1b[:, bass.ts(p.index, D)], x1[p.place][:, :], bo_bc[:, :],
                                            ALU.add).then_inc(x1b_ready, 1)
                if w:
                    root(mv2[:, 1:2], ve2, var2_ready, ve2_ready, rstd2, rstd2_ready, w)
                if p:
                    pool.wait_ge(rope_ready, p.done)
                    wait_before(pool, sc_ready, p, 2)
                    nc.gpsimd.tensor_tensor(qkt[p.place][:, :], rope_c[:, :], rope_s[:, :], ALU.add).then_inc(qk_ready, 1)
                if a:
                    root(mv1[:, 1:2], ve1, var1_ready, ve1_ready, rstd1, rstd1_ready, a)
                if q:
                    pool.wait_ge(scmax_ready, q.done)
                    wait_before(pool, pb_ready, q)
                    nc.gpsimd.tensor_tensor(sd_sb[:, :, :], sc_sb[:, :, :], spread(sc_max[:, :], 2, [P, HEADS, S]),
                                            ALU.subtract).then_inc(sd_ready, 1)

            def gather(j):
                wait_before(pool, xb_ready, j, RING)
                pool.wait_ge(from_copied, j.done)
                carry(pool, pool_passed)
                pool.indirect_dma_start(xs[j.place][:, :], None, x2_dram,
                                        bass.IndirectOffsetOnAxis(from_cur[j.place][:, :], 0)
                                        ).then_inc(xs_in[j.place], 16)

            def expert_slot(x, h, y, done, ahead):
                if ahead and not (isinstance(ahead.index, int) and ahead.index < RING):
                    gather(ahead)
                if y:
                    pool.wait_ge(ve3_ready, y.done)
                    nc.gpsimd.tensor_tensor(rstd3[y.place % 2][:, :], ve3[y.place % 2][:, :], half_neg[:, :],
                                            ALU.pow).then_inc(rstd3_ready, 1)
                if done:
                    pool.wait_ge(to_copied, done.done)
                    pool.wait_ge(res_ready, done.done)
                    carry(pool, pool_passed)
                    pool.indirect_dma_start(out, bass.IndirectOffsetOnAxis(to_cur[done.place][:, :], 0),
                                            res[done.place][:, :], None, bounds_check=NT * P - 1, oob_is_err=False
                                            ).then_inc(out_stored[done.place], 16)

            nc.gpsimd.memset(half_neg[:, :], -0.5).then_inc(pool_setup, 1)
            nc.gpsimd.memset(ones_bf[:, :], 1.0).then_inc(pool_ones, 1)
            pool.wait_ge(pool_setup, 1)
            pool.wait_ge(table_in, 1)
            pipeline(pool, slot)
            pool.wait_ge(tile_hot_ready, 1)
            pool.wait_ge(vals_ready, 1)
            nc.gpsimd.tensor_tensor(tile_vals[:, 0:POOL_VALS], spread(tile_hot[:, 0:POOL_VALS, :], 2,
                                                                      [P, POOL_VALS, VALS, FT]),
                                    spread(vals[:, 0:POOL_VALS, :], 3, [P, POOL_VALS, VALS, FT]),
                                    ALU.mult).then_inc(pool_vals_ready, 1)
            for n in range(2):
                pool.wait_ge(x2_stored[n], NT // 2 * 16)
            for n in range(RING):
                gather(Tile(0, n, RING))
            expert_pipeline(pool, expert_slot)
            for n in range(RING):
                pool.wait_ge(out_stored[n], len(range(n, FT, RING)) * 16)


_IN = ["x_tok", "x_t", "x_scale", "ctx_t", "mask", "attn_kt", "attn_v", "wq", "wq_swap", "wk", "wk_swap", "wv", "wo",
       "bo", "router_w", "router_b", "w1", "b1", "w2", "b2", "consts"]


def _constants():
    import numpy as np

    c = np.zeros((P, C_ALL), np.float32)
    c[:, C_ID:C_ID + P] = np.eye(P)
    inv_freq = (1.0 / np.float32(10000.0) ** (np.arange(0, HD, 2, dtype=np.float32) / np.float32(HD))).astype(np.float32)
    angle = (np.arange(S, dtype=np.float32)[:, None] * inv_freq[None, :]).astype(np.float32)
    feature = np.arange(P)
    pair = (feature % HD) // 2
    cos, sin = np.cos(angle)[:, pair].T, np.sin(angle)[:, pair].T
    sin = sin * np.where(feature % 2 == 0, -1.0, 1.0)[:, None]
    root = np.float32(1.0 / np.sqrt(HD))
    for n in range(2):
        c[:, C_COS + n * S:C_COS + (n + 1) * S] = cos * root
        c[:, C_COS + P + n * S:C_COS + P + (n + 1) * S] = cos
        c[:, C_SIN + n * S:C_SIN + (n + 1) * S] = sin * root
        c[:, C_SIN + P + n * S:C_SIN + P + (n + 1) * S] = sin
    c[feature, C_HM + (feature // HD) % HG] = 1.0
    for n in range(2):
        for m in range(2):
            col = C_OWN + (m * 2 + m) * PD + n * HD
            c[n * S:(n + 1) * S, col:col + HD] = 1.0
    c[:, C_TRI:C_TRI + P] = feature[:, None] < feature[None, :]
    c[:, C_IOTA:C_IOTA + P] = feature[None, :]
    c[:, C_W8:C_W8 + E] = E - np.arange(E)[None, :]
    tok = np.zeros((P, NT, 2), np.float32)
    tok[:, :, 0] = np.arange(NT)[None, :]
    tok[:, :, 1] = feature[:, None]
    c[:, C_TOK:C_TOK + 2 * NT] = tok.reshape(P, -1)
    expert = np.arange(E)
    c[:, C_LT:C_LT + E * E] = (P * (expert[None, :] < expert[:, None])).reshape(1, -1)
    c[:, C_LE:C_LE + E * E] = (expert[None, :] <= expert[:, None]).reshape(1, -1)
    return c


def kernel(**inputs):
    import numpy as np
    import concourse.bacc as bacc
    from concourse.bass_utils import run_bass_kernel_spmd

    i = {k: np.asarray(v) for k, v in inputs.items()}
    x = i["x"].reshape(NT * P, D)
    swap = np.arange(D) ^ 1
    wo = np.zeros((CG, 2, PD, 2, OCT, D), i["L0_xattn_Wo"].dtype)
    for n in range(2):
        wo[:, n, :, n] = i["L0_xattn_Wo"].reshape(OCT, CG, PD, D).transpose(1, 2, 0, 3)
    arrays = {
        "x_tok": x,
        "x_t": x.T,
        "x_scale": i["x"][:, ::S // 4, :].reshape(B, T),
        "ctx_t": i["ctx_1024"].reshape(NT * P, D).T,
        "mask": i["mask_Bx1xSxS2_ik1"].reshape(NT * P, S),
        "attn_kt": i["L0_attn_k"][0].T,
        "attn_v": i["L0_attn_v"][0].reshape(TB, P, D).transpose(1, 0, 2),
        "wq": i["L0_xattn_Wq"], "wq_swap": i["L0_xattn_Wq"][:, swap],
        "wk": i["L0_xattn_Wk"], "wk_swap": i["L0_xattn_Wk"][:, swap],
        "wv": i["L0_xattn_Wv"].reshape(D, HPAIR, 2, HD).transpose(0, 2, 1, 3).reshape(D, D),
        "wo": wo.reshape(P, 2 * OCT * D), "bo": i["L0_xattn_bo"].reshape(1, D),
        "router_w": i["L0_ffn_router_W"], "router_b": i["L0_ffn_router_b"].reshape(1, E),
        "w1": i["L0_ffn_W1"].transpose(1, 0, 2).reshape(P, E * F),
        "b1": i["L0_ffn_b1"].reshape(E, FB, P).transpose(2, 0, 1).reshape(P, E * FB),
        "w2": i["L0_ffn_W2"].reshape(E, FB, P, D).transpose(2, 0, 1, 3).reshape(P, E * FB * D),
        "b2": i["L0_ffn_b2"].reshape(1, E * D),
        "consts": _constants(),
    }
    nc = bacc.Bacc("TRN2", target_bir_lowering=False, num_devices=1)
    feeds, args = {}, []
    for name in _IN:
        a = np.ascontiguousarray(arrays[name])
        feeds[f"in_{name}"] = a
        args.append(nc.dram_tensor(f"in_{name}", a.shape, mybir.dt.from_np(a.dtype), kind="ExternalInput").ap())
    result = nc.dram_tensor("out", (NT * P, D), F32, kind="ExternalOutput").ap()
    decoder_kernel(nc, *args, result)
    r = run_bass_kernel_spmd(nc, [feeds], core_ids=[0])
    return np.asarray(r.results[0]["out"]).reshape(B, S, D)
```
